# Optimizing a Trainium2 kernel written in Bass

```python
import numpy as np
import jax
import jax.numpy as jnp

def _softmax(x, axis=-1):
    return jax.nn.softmax(x, axis=axis)

def _gelu(x):
    return jax.nn.gelu(x, approximate=True)

def _silu(x):
    return jax.nn.silu(x)

def _sigmoid(x):
    return jax.nn.sigmoid(x)

def _layernorm(x, axis=-1, eps=1e-05):
    m = jnp.mean(x, axis=axis, keepdims=True)
    v = jnp.var(x, axis=axis, keepdims=True)
    return (x - m) / jnp.sqrt(v + eps)

def _scatter_add(tgt, idx, src, axis=0):
    return tgt.at[idx].add(src)

def _segment_sum(src, seg, n):
    return jax.ops.segment_sum(src, seg, n)
kernel_name = 'mk_gnn_resnorm_d1_gnn_r8_758347'

def setup_inputs(seed: int=0):
    np.random.seed(seed)
    _w = jnp.asarray

    def _rec_inputs():
        import jax
        import jax.numpy as jnp
        _gk = jax.random.key(seed)
        x = -0.000202 + 1 * jax.random.normal(jax.random.fold_in(_gk, 1), (12500, 64), jnp.float32)
        _s = jax.random.randint(jax.random.fold_in(_gk, 2), (100000,), 0, 12500, jnp.int32)
        _d = jax.random.randint(jax.random.fold_in(_gk, 3), (100000,), 0, 12500, jnp.int32)
        _loop = jnp.arange(12500, dtype=jnp.int32)
        src = jnp.concatenate([_s, _d, _loop])
        dst = jnp.concatenate([_d, _s, _loop])
        _o = jnp.argsort(dst, stable=True)
        src = src[_o]
        dst = dst[_o]
        edge_attr_32 = -5.16925e-05 + 1.00005 * jax.random.normal(jax.random.fold_in(_gk, 12), (212500, 32), jnp.float32)
        return (x, src, dst, edge_attr_32)
    x, src, dst, edge_attr_32 = _rec_inputs()

    def _L0_gnn_setup():
        import jax, jax.numpy as jnp
        import numpy as np
        N_NODES = 12500
        N_EDGES = 400000
        EDGE_OUT = 32
        HID = 128
        NODE_OUT = 64
        N_GRAPHS = 16
        key = jax.random.key(seed)
        ks = jax.random.split(key, 9)
        x = jax.random.normal(ks[0], (N_NODES, 64), dtype=jnp.float32)
        edge_index = jax.random.randint(ks[1], (2, N_EDGES), 0, N_NODES, dtype=jnp.int64)
        edge_attr = jax.random.normal(ks[2], (N_EDGES, EDGE_OUT), dtype=jnp.float32)
        u = jax.random.normal(ks[3], (N_GRAPHS, 1), dtype=jnp.float32)
        batch = jnp.sort(jax.random.randint(ks[4], (N_NODES,), 0, N_GRAPHS, dtype=jnp.int64))
        d_in = 3 * EDGE_OUT + 1
        W1 = jax.random.normal(ks[5], (d_in, HID), dtype=jnp.float32) / np.sqrt(d_in)
        b1 = jnp.zeros((HID,), dtype=jnp.float32)
        W2 = jax.random.normal(ks[6], (HID, NODE_OUT), dtype=jnp.float32) / np.sqrt(HID)
        b2 = jnp.zeros((NODE_OUT,), dtype=jnp.float32)
        return {'x': x, 'edge_index': edge_index, 'edge_attr': edge_attr, 'u': u, 'batch': batch, 'W1': W1, 'b1': b1, 'W2': W2, 'b2': b2}
    _L0_gnn_all = _L0_gnn_setup()
    _L0_gnn_in = {k: v for k, v in _L0_gnn_all.items() if k in ('u', 'W1', 'b1', 'W2', 'b2')}
    del _L0_gnn_all
    return {'x': x, 'src': src, 'dst': dst, 'edge_attr_32': edge_attr_32, 'L0_gnn_u': _L0_gnn_in['u'], 'L0_gnn_W1': _L0_gnn_in['W1'], 'L0_gnn_b1': _L0_gnn_in['b1'], 'L0_gnn_W2': _L0_gnn_in['W2'], 'L0_gnn_b2': _L0_gnn_in['b2']}

def reference(x, src, dst, edge_attr_32, L0_gnn_u, L0_gnn_W1, L0_gnn_b1, L0_gnn_W2, L0_gnn_b2):
    import jax
    import jax.numpy as jnp

    def _L0_gnn_ref(x, edge_index, edge_attr, u, batch, W1, b1, W2, b2):
        import jax, jax.numpy as jnp
        import numpy as np
        N_NODES = 12500
        N_EDGES = 400000
        EDGE_OUT = 32
        HID = 128
        NODE_OUT = 64
        N_GRAPHS = 16
        N = x.shape[0]
        row = edge_index[0]
        seg_sum = jax.ops.segment_sum(edge_attr, row, num_segments=N)
        seg_max = jax.ops.segment_max(edge_attr, row, num_segments=N)
        cnt = jax.ops.segment_sum(jnp.ones((edge_attr.shape[0], 1), edge_attr.dtype), row, num_segments=N)
        seg_mean = seg_sum / jnp.maximum(cnt, 1.0)
        seg_max = jnp.where(cnt > 0, seg_max, 0.0)
        h = jnp.concatenate([seg_sum, seg_max, seg_mean, u[batch]], axis=1)
        h = jax.nn.relu(h @ W1 + b1)
        return h @ W2 + b2
    edge_index = jnp.stack([src, dst])
    batch0 = jnp.zeros((12500,), jnp.int32)
    x = _layernorm(x + _L0_gnn_ref(x, edge_index, edge_attr_32, L0_gnn_u, batch0, L0_gnn_W1, L0_gnn_b1, L0_gnn_W2, L0_gnn_b2), axis=-1)
    return x

_drawn_inputs = setup_inputs


def setup_inputs(seed=0):
    import zlib

    import numpy as np

    out = dict(_drawn_inputs(seed))
    spreads = {'L0_gnn_b1': (0.0, 0.1), 'L0_gnn_b2': (0.0, 0.1)}
    factors = {}
    for name, (base, spread) in spreads.items():
        noise = np.random.default_rng([zlib.crc32(name.encode()), seed]).standard_normal(out[name].shape)
        drawn = base * np.exp(spread * noise) if base else spread * noise
        out[name] = jnp.asarray(drawn.astype(out[name].dtype))
    for name, factor in factors.items():
        out[name] = (out[name] * factor).astype(out[name].dtype)
    return out
```

```python
import concourse.bass as bass
from concourse import mybir
from contextlib import ExitStack

P = 128
FLT_MAX = 3.4028234663852886e38


def gnn_kernel(nc, x, src, edge, u, W1, b1, W2, b2, out):
    f32, bf16 = mybir.dt.float32, mybir.dt.bfloat16
    i32, i16 = mybir.dt.int32, mybir.dt.int16
    ALU = mybir.AluOpType
    ACT = mybir.ActivationFunctionType
    AX = mybir.AxisListType

    N, D = x.shape
    E, F = edge.shape
    H = W1.shape[1]
    NT = -(-N // P)
    NLAST = N - (NT - 1) * P
    ET = E // P
    EREST = E - ET * P
    K = 4
    STEPS = -(-(ET + 1) // K)
    J = 4
    ROUNDS = STEPS // J
    COLS = STEPS * K
    assert ROUNDS * J == STEPS and (STEPS - 1) * K == ET
    NOHI = NT
    R = COLS
    ROWS = P * R
    SPARE = ROWS
    ZROW = ROWS + P
    CH = 128
    NCH = R // CH
    G = 7
    GROUPS = NT // G
    assert GROUPS * G == NT and NCH * CH == R and NCH % 2 and GROUPS % 2 == 0
    assert EREST <= P and ET % K == 0

    rows_dram = nc.dram_tensor("sorted_rows", [ROWS, F], f32, kind="Internal").ap()
    scan_dram = nc.dram_tensor("scanned_rows", [ROWS + 2 * P, 2 * F], f32, kind="Internal").ap()

    ctx = ExitStack()
    with ctx:
        def sb(name, shape, dt):
            return ctx.enter_context(nc.sbuf_tensor(name, shape, dt))

        def pb(name, shape, dt):
            return ctx.enter_context(nc.psum_tensor(name, shape, dt))

        def sem(name):
            return ctx.enter_context(nc.semaphore(name))

        idf = sb("idf", [P, P], f32)
        idb = sb("idb", [P, P], bf16)
        iota32 = sb("iota32", [P, R], i32)
        iota16 = sb("iota16", [P, R], i16)
        iota_b = sb("iota_b", [P, P], bf16)
        before = sb("before", [P, P], f32)
        late = sb("late", [P, K, P], bf16)
        prow = sb("prow", [P, 1], i32)
        prowf = sb("prowf", [P, 1], f32)
        zeros = sb("zeros", [P, P], f32)
        w1 = sb("w1", [3 * F, H], f32)
        w1u = sb("w1u", [P, 1], f32)
        ucol = sb("ucol", [P, 1], f32)
        b1c = sb("b1c", [P, 1], f32)
        bias1 = sb("bias1", [P, 1], f32)
        w2 = sb("w2", [H, D], f32)
        b2b = sb("b2b", [P, D], f32)
        srck = sb("srck", [P, COLS], i32)
        ki = sb("ki", [P, COLS], i32)
        keys = sb("keys", [P, 2, COLS], f32)
        kb = sb("kb", [P, J, 2, K], f32)
        oh_lo = sb("oh_lo", [P, J, K, P], bf16)
        oh_hi = sb("oh_hi", [P, J, K, NT], bf16)
        loT = sb("loT", [P, 2, K, P], bf16)
        loTf = sb("loTf", [P, 2, K, P], f32)
        earlier = sb("earlier", [P, 2, K, P], bf16)
        table = sb("table", [P, 2, NT], f32)
        picked = sb("picked", [P, K, NT], f32)
        posf = sb("posf", [P, 2, K], f32)
        pos = sb("pos", [P, J, K], i32)
        feat = sb("feat", [P, J, K, F], f32)
        cnt = sb("cnt", [P, NT], f32)
        incl = sb("incl", [P, NT], f32)
        start = sb("start", [P, NT], f32)
        quo = sb("quo", [P, NT], f32)
        rem = sb("rem", [P, NT], f32)
        tmpn = sb("tmpn", [P, NT], f32)
        rcnt = sb("rcnt", [P, NT], f32)
        endf = sb("endf", [P, NT], f32)
        endi = sb("endi", [P, NT], i32)
        off = sb("off", [P, 1], f32)
        ohq = sb("ohq", [P, 2, P], bf16)
        ohr = sb("ohr", [P, 2, R], bf16)
        keep = sb("keep", [P, R], f32)
        keepm = sb("keepm", [P, R], f32)
        xs = sb("xs", [P, 2, CH, F], f32)
        sc = sb("sc", [P, 2, CH, 2 * F], f32)
        t1 = sb("t1", [P, 8], f32)
        fixi = sb("fixi", [P, 1], i32)
        nf = sb("nf", [P, 2 * F], f32)
        tailT = sb("tailT", [2 * F, P], f32)
        nfT = sb("nfT", [2 * F, P], f32)
        chain = sb("chain", [2 * F, P + 1], f32)
        carry = sb("carry", [P, 2 * F], f32)
        fixg = sb("fixg", [P, 2 * F], f32)
        fixo = sb("fixo", [P, 2 * F], f32)
        xn = sb("xn", [P, NT, D], f32)
        gi = sb("gi", [P, 2, G], i32)
        flat = xs[:].rearrange("p a b c -> p (a b c)")
        h = flat[:, 0:2 * G * 3 * F].rearrange("p (a g f) -> p a g f", a=2, g=G)
        y = flat[:, 2048:2048 + 2 * G * D].rearrange("p (a g f) -> p a g f", a=2, g=G)
        hT = flat[0:3 * F, 4096:4096 + G * P].rearrange("p (g n) -> p g n", g=G)
        r1 = flat[:, 6144:6144 + G * P].rearrange("p (g n) -> p g n", g=G)
        assert 2 * G * 3 * F <= 2048 and 2 * G * D <= 2048 and G * P <= 2048
        st = sb("st", [P, 2, G, 6], f32)
        mv = sb("mv", [P, 2, G, 2], f32)
        sd = sb("sd", [P, 2, G], f32)
        rs = sb("rs", [P, 2, G], f32)

        banks = pb("banks", [P, 8, 512], f32)
        pC = banks[:, 0, :]
        C = pC[:, 0:NT]
        pG = banks[:, 1:3, :]
        pE = [banks[:, b, :].rearrange("p (k n) -> p k n", k=K) for b in (3, 7)]
        pT = [banks[:, b, :].bitcast(bf16)[:, 0:K * P].rearrange("p (k n) -> p k n", k=K) for b in (4, 5)]
        pF = banks[:, 4:8, :]

        s_const = sem("s_const")
        s_castc = sem("s_castc")
        s_src = sem("s_src")
        s_fill = sem("s_fill")
        s_w = sem("s_w")
        s_xn = sem("s_xn")
        s_xz = sem("s_xz")
        s_init = sem("s_init")
        s_keys = sem("s_keys")
        s_kb1 = sem("s_kb1")
        s_oh1 = sem("s_oh1")
        s_cnt = sem("s_cnt")
        s_tot = sem("s_tot")
        s_off = sem("s_off")
        s_start = sem("s_start")
        s_node = sem("s_node")
        s_kb = sem("s_kb")
        s_oh = sem("s_oh")
        s_T = sem("s_T")
        s_loT = sem("s_loT")
        s_loTf = sem("s_loTf")
        s_eq = sem("s_eq")
        s_earl = sem("s_earl")
        s_C = sem("s_C")
        s_tab = sem("s_tab")
        s_G = sem("s_G")
        s_pick = sem("s_pick")
        s_pos = sem("s_pos")
        s_feat = [sem(f"s_feat{j}") for j in range(J)]
        s_scat = [sem(f"s_scat{j}") for j in range(J)]
        s_ohr = sem("s_ohr")
        s_flag = sem("s_flag")
        s_keepm = sem("s_keepm")
        s_end = sem("s_end")
        s_xs = [sem(f"s_xs{b}") for b in range(2)]
        s_sc = sem("s_sc")
        s_so = [sem(f"s_so{b}") for b in range(2)]
        s_nf = sem("s_nf")
        s_trT = sem("s_trT")
        s_ch = sem("s_ch")
        s_cT = sem("s_cT")
        s_fi = sem("s_fi")
        s_fg = sem("s_fg")
        s_fo = sem("s_fo")
        s_fs = sem("s_fs")
        s_v = sem("s_v")
        s_gi = sem("s_gi")
        s_g = [sem(f"s_g{b}") for b in range(2)]
        s_mean = sem("s_mean")
        s_hT = sem("s_hT")
        s_hTc = sem("s_hTc")
        s_l1 = sem("s_l1")
        s_r1 = sem("s_r1")
        s_l2 = sem("s_l2")
        s_y = sem("s_y")
        s_st = sem("s_st")
        s_mv = sem("s_mv")
        s_ve = sem("s_ve")
        s_sd = sem("s_sd")
        s_rs = sem("s_rs")
        s_yn = sem("s_yn")
        s_out = [sem(f"s_out{b}") for b in range(2)]

        block = ctx.enter_context(nc.Block())

        edge_t = edge[0:ET * P, :].rearrange("(p t) f -> p t f", t=ET)
        rows_p = rows_dram.rearrange("(p r) f -> p r f", r=R)
        scan_p = scan_dram[0:ROWS, :].rearrange("(p r) f -> p r f", r=R)
        x_t = x[0:(NT - 1) * P, :].rearrange("(t p) d -> p t d", p=P)
        out_t = out[0:(NT - 1) * P, :].rearrange("(t p) d -> p t d", p=P)

        @block.sync
        def _(sp):
            sp.dma_start(srck[:, 0:ET], src[0:ET * P].rearrange("(p t) -> p t", t=ET)).then_inc(s_src, 16)
            sp.wait_ge(s_fill, 1)
            sp.dma_start(srck[0:EREST, ET:ET + 1],
                         src[ET * P:E].rearrange("(p o) -> p o", o=1)).then_inc(s_src, 16)

            def load_rows(i, j):
                if not (isinstance(i, int) and i == 0):
                    sp.wait_ge(s_scat[j], 16 * K * i)
                sp.dma_start(feat[:, j, :, :],
                             edge_t[:, bass.ds(K * (J * i + j), K), :]).then_inc(s_feat[j], 16)

            for j in range(J):
                load_rows(0, j)
            sp.dma_start(w1[:], W1[0:3 * F, :]).then_inc(s_w, 16)
            sp.dma_start(w1u[:], W1[3 * F:3 * F + 1, :].rearrange("o h -> h o")).then_inc(s_w, 16)
            sp.dma_start(ucol[:], u[0:1, 0:1].to_broadcast([P, 1])).then_inc(s_w, 16)
            sp.dma_start(b1c[:], b1.rearrange("(h o) -> h o", o=1)).then_inc(s_w, 16)
            sp.dma_start(w2[:], W2).then_inc(s_w, 16)
            sp.dma_start(b2b[:], b2.rearrange("(o d) -> o d", o=1).to_broadcast([P, D])).then_inc(s_w, 16)
            sp.wait_ge(s_const, 1)
            pad = ROWS - E
            part = pad // 4
            sp.dma_start(rows_dram[E:ROWS, :].rearrange("(p k) f -> p (k f)", k=4),
                         zeros[0:part, 0:4 * F]).then_inc(s_init, 16)
            sp.dma_start(scan_dram[ROWS:ROWS + 2 * P, :].rearrange("(p k) f -> p (k f)", k=2),
                         zeros[:, 0:4 * F]).then_inc(s_init, 16)
            with sp.Fori(1, ROUNDS - 1) as i:
                for j in range(J):
                    load_rows(i, j)
            for j in range(J - 1):
                load_rows(ROUNDS - 1, j)
            j = J - 1
            sp.wait_ge(s_scat[j], 16 * K * (ROUNDS - 1))
            sp.dma_start(feat[0:EREST, j, 0, :], edge[ET * P:E, :]).then_inc(s_feat[j], 16)
            sp.wait_ge(s_xz, 1)
            sp.dma_start(xn[:, 0:NT - 1, :], x_t).then_inc(s_xn, 16)
            sp.dma_start(xn[0:NLAST, NT - 1, :], x[(NT - 1) * P:N, :]).then_inc(s_xn, 16)

            sp.wait_ge(s_init, 32)
            for j in range(J):
                sp.wait_ge(s_scat[j], 16 * K * ROUNDS if j < J - 1 else 16 * (K * (ROUNDS - 1) + 1))

            def load_chunk(k, b):
                sp.dma_start(xs[:, b, :, :], rows_p[:, bass.ds(k * CH, CH), :]).then_inc(s_xs[b], 16)

            def store_chunk(k, b):
                sp.wait_ge(s_sc, k + 1)
                sp.dma_start(scan_p[:, bass.ds(k * CH, CH), :], sc[:, b, :, :]).then_inc(s_so[b], 16)

            load_chunk(0, 0)
            load_chunk(1, 1)
            store_chunk(0, 0)
            load_chunk(2, 0)
            with sp.Fori(0, NCH // 2 - 1) as m:
                store_chunk(2 * m + 1, 1)
                load_chunk(2 * m + 3, 1)
                store_chunk(2 * m + 2, 0)
                load_chunk(2 * m + 4, 0)
            store_chunk(NCH - 2, 1)
            store_chunk(NCH - 1, 0)

            def store_group(g, b):
                sp.wait_ge(s_yn, g + 1)
                sp.dma_start(out_t[:, bass.ds(g * G, G), :], y[:, b, :, :]).then_inc(s_out[b], 16)

            with sp.Fori(0, GROUPS // 2 - 1) as m:
                store_group(2 * m, 0)
                store_group(2 * m + 1, 1)
            store_group(GROUPS - 2, 0)
            sp.wait_ge(s_yn, GROUPS)
            sp.dma_start(out_t[:, NT - G:NT - 1, :], y[:, 1, 0:G - 1, :]).then_inc(s_out[1], 16)
            sp.dma_start(out[(NT - 1) * P:N, :], y[0:NLAST, 1, G - 1, :]).then_inc(s_out[1], 16)
            sp.wait_ge(s_out[0], 16 * (GROUPS // 2))
            sp.wait_ge(s_out[1], 16 * (GROUPS // 2 + 1))

        @block.gpsimd
        def _(g):
            nc.gpsimd.memset(zeros[:], 0.0).then_inc(s_const, 1)
            g.iota(iota32[:], pattern=[[1, R]], base=0, channel_multiplier=0).then_inc(s_const, 1)
            g.iota(prow[:], pattern=[[1, 1]], base=0, channel_multiplier=1).then_inc(s_const, 1)
            nc.gpsimd.memset(idf[:], 0.0).then_inc(s_const, 1)
            nc.gpsimd.memset(before[:], 1.0).then_inc(s_const, 1)
            nc.gpsimd.memset(late[:], -1.0).then_inc(s_const, 1)
            g.wait_ge(s_const, 6)
            g.affine_select(out=idf[:], in_=idf[:], compare_op=ALU.not_equal, fill=1.0, base=0,
                            pattern=[[-1, P]], channel_multiplier=1).then_inc(s_const, 1)
            g.affine_select(out=before[:], in_=before[:], compare_op=ALU.is_gt, fill=0.0, base=0,
                            pattern=[[1, P]], channel_multiplier=-1).then_inc(s_const, 1)
            g.affine_select(out=late[:], in_=late[:], compare_op=ALU.is_ge, fill=0.0, base=0,
                            pattern=[[0, K], [-1, P]], channel_multiplier=1).then_inc(s_const, 1)
            nc.gpsimd.memset(xn[:, NT - 1, :], 0.0).then_inc(s_xz, 1)

            def scatter(i, j, tiles, parts):
                g.wait_ge(s_feat[j], 16 * (i + 1))
                g.wait_ge(s_pos, J * i + j + 1)
                g.nop(nofuse=True)
                for k in range(tiles):
                    g.indirect_dma_start(rows_dram, bass.IndirectOffsetOnAxis(pos[0:parts, j, k:k + 1], 0),
                                         feat[0:parts, j, k, :], None).then_inc(s_scat[j], 16)

            with g.Fori(0, ROUNDS - 1) as i:
                for j in range(J):
                    scatter(i, j, K, P)
            for j in range(J - 1):
                scatter(ROUNDS - 1, j, K, P)
            scatter(ROUNDS - 1, J - 1, 1, EREST)

            g.wait_ge(s_keepm, 1)
            g.affine_select(out=keep[:], in_=keep[:], compare_op=ALU.not_equal, fill=0.0, base=-E,
                            pattern=[[1, R]], channel_multiplier=R).then_inc(s_end, 1)

            g.wait_ge(s_fi, 1)
            g.wait_ge(s_so[0], 16 * (NCH // 2 + 1))
            g.wait_ge(s_so[1], 16 * (NCH // 2))
            g.indirect_dma_start(fixg[:], None, scan_dram, bass.IndirectOffsetOnAxis(fixi[:, 0:1], 0)).then_inc(s_fg, 16)
            g.wait_ge(s_fo, 1)
            g.indirect_dma_start(scan_dram, bass.IndirectOffsetOnAxis(fixi[:, 0:1], 0), fixo[:], None).then_inc(s_fs, 16)
            g.wait_ge(s_fs, 16)

            def gather(q, b):
                if not (isinstance(q, int) and q < 2):
                    g.wait_ge(s_hT, q - 1)
                g.wait_ge(s_gi, q + 1)
                g.nop(nofuse=True)
                for k in range(G):
                    g.indirect_dma_start(h[:, b, k, 0:2 * F], None, scan_dram,
                                         bass.IndirectOffsetOnAxis(gi[:, b, k:k + 1], 0)).then_inc(s_g[b], 16)

            gather(0, 0)
            gather(1, 1)
            with g.Fori(1, GROUPS // 2) as m:
                gather(2 * m, 0)
                gather(2 * m + 1, 1)

        @block.vector
        def _(v):
            order = [0]

            def then(ins):
                order[0] += 1
                ins.then_inc(s_v, 1)
                v.wait_ge(s_v, order[0])

            nc.vector.memset(srck[:, ET:COLS], NOHI * P).then_inc(s_fill, 1)
            v.wait_ge(s_const, 9)
            nc.vector.tensor_copy(iota_b[:], iota32[:, 0:P]).then_inc(s_castc, 1)
            nc.vector.tensor_copy(iota16[:], iota32[:]).then_inc(s_castc, 1)
            nc.vector.tensor_copy(idb[:], idf[:]).then_inc(s_castc, 1)
            nc.vector.tensor_copy(prowf[:], prow[:]).then_inc(s_castc, 1)
            v.wait_ge(s_src, 32)
            then(nc.vector.tensor_single_scalar(ki[:], srck[:], P - 1, op=ALU.bitwise_and))
            nc.vector.tensor_copy(keys[:, 0, :], ki[:]).then_inc(s_keys, 1)
            v.wait_ge(s_keys, 1)
            then(nc.vector.tensor_single_scalar(ki[:], srck[:], 7, op=ALU.arith_shift_right))
            nc.vector.tensor_copy(keys[:, 1, :], ki[:]).then_inc(s_keys, 1)
            v.wait_ge(s_keys, 2)
            v.wait_ge(s_castc, 4)

            def one_hots(j, done):
                for k in range(K):
                    nc.vector.tensor_scalar(oh_lo[:, j, k, :], iota_b[:], kb[:, j, 0, k:k + 1], None, ALU.is_equal)
                for k in range(K):
                    last = nc.vector.tensor_scalar(oh_hi[:, j, k, :], iota_b[:, 0:NT], kb[:, j, 1, k:k + 1], None,
                                                   ALU.is_equal)
                last.then_inc(done, 1)

            def copy_keys(s, j, done):
                nc.vector.tensor_copy(kb[:, j, :, :], keys[:, :, bass.ds(K * s, K)]).then_inc(done, 1)

            def count_round(i):
                for j in range(J):
                    if not (isinstance(i, int) and i == 0):
                        v.wait_ge(s_oh1, J * (i - 1) + j + 1)
                    copy_keys(J * i + j, j, s_kb1)
                for j in range(J):
                    v.wait_ge(s_kb1, J * i + j + 1)
                    if not (isinstance(i, int) and i == 0):
                        v.wait_ge(s_cnt, J * (i - 1) + j + 1)
                    one_hots(j, s_oh1)

            count_round(0)
            with v.Fori(1, ROUNDS) as i:
                count_round(i)

            v.wait_ge(s_cnt, STEPS)
            then(nc.vector.tensor_copy(cnt[:], C))
            then(nc.vector.memset(tmpn[:], 1.0))
            nc.vector.tensor_tensor_scan(incl[:], tmpn[:], cnt[:], 0.0, ALU.mult, ALU.add).then_inc(s_tot, 1)
            v.wait_ge(s_off, 1)
            v.wait_ge(s_tot, 1)
            then(nc.vector.tensor_copy(off[:], pG[:, 0, 0:1]))
            then(nc.vector.tensor_tensor(start[:], incl[:], cnt[:], ALU.subtract))
            nc.vector.tensor_scalar(start[:], start[:], off[:, 0:1], None, ALU.add).then_inc(s_start, 1)
            v.wait_ge(s_start, 1)

            def prepare(s, j, i0):
                v.wait_ge(s_kb, s + 1)
                if not i0:
                    v.wait_ge(s_C, K * (s - J) + K + 1)
                    v.wait_ge(s_pick, K * (s - J) + K)
                one_hots(j, s_oh)

            def pick(s, j, first):
                for k in range(K):
                    if not first:
                        v.wait_ge(s_pick, K * (s - 1) + k + 1)
                        if k == 0 and not (isinstance(s, int) and s < 2):
                            v.wait_ge(s_pos, s - 1)
                    v.wait_ge(s_G, K * s + k + 1)
                    nc.vector.scalar_tensor_tensor(
                        out=picked[:, k, :], in0=pG[:, k % 2, 0:NT], scalar=1.0, in1=oh_hi[:, j, k, :],
                        op0=ALU.mult, op1=ALU.mult, accum_out=posf[:, j % 2, k:k + 1]).then_inc(s_pick, 1)

            def to_int(s, j, i):
                v.wait_ge(s_pick, K * (s + 1))
                if not (isinstance(i, int) and i == 0):
                    v.wait_ge(s_scat[j], 16 * K * i)
                nc.vector.tensor_copy(pos[:, j, :], posf[:, j % 2, :]).then_inc(s_pos, 1)

            def flag_column(c, b, first):
                if not first:
                    v.wait_ge(s_flag, c - 1)
                nc.vector.tensor_scalar(ohq[:, b, :], iota_b[:], quo[:, bass.ds(c, 1)], None, ALU.is_equal)
                nc.vector.tensor_scalar(ohr[:, b, :], iota16[:], rem[:, bass.ds(c, 1)], None,
                                        ALU.is_equal).then_inc(s_ohr, 1)

            def sort_round(i, first=False, last=False):
                for j in range(J):
                    s = J * i + j
                    if not (last and j + 3 >= J):
                        if not (first and j == 0):
                            v.wait_ge(s_oh, s)
                        copy_keys(s + 3, (j + 3) % J, s_kb)
                    if not (last and j + 2 >= J):
                        prepare(s + 2, (j + 2) % J, first and j + 2 < J)
                    pick(s, j, first and j == 0)
                    to_int(s, j, i)

            for s in range(3):
                copy_keys(s, s, s_kb)
            for s in range(2):
                prepare(s, s, True)
            then(nc.vector.tensor_scalar(quo[:], start[:], 1.0 / R, 0.5 / R - 0.5, ALU.mult, ALU.add))
            then(nc.vector.tensor_scalar(quo[:], quo[:], 12582912.0, 12582912.0, ALU.add, ALU.subtract))
            then(nc.vector.scalar_tensor_tensor(out=rem[:], in0=quo[:], scalar=-float(R), in1=start[:],
                                                op0=ALU.mult, op1=ALU.add))
            then(nc.vector.tensor_scalar(rcnt[:], cnt[:], 1.0, None, ALU.max))
            then(nc.vector.reciprocal(rcnt[:], rcnt[:]))
            then(nc.vector.scalar_tensor_tensor(out=endf[:], in0=cnt[:], scalar=-1.0 - ZROW, in1=start[:],
                                                op0=ALU.add, op1=ALU.add))
            then(nc.vector.tensor_scalar(tmpn[:], cnt[:], 0.0, None, ALU.is_gt))
            then(nc.vector.tensor_tensor(endf[:], endf[:], tmpn[:], ALU.mult))
            then(nc.vector.tensor_scalar(endf[:], endf[:], float(ZROW), None, ALU.add))
            then(nc.vector.tensor_copy(endi[:], endf[:]))
            v.wait_ge(s_w, 96)
            then(nc.vector.tensor_scalar(bias1[:], w1u[:], ucol[:, 0:1], b1c[:, 0:1], ALU.mult, ALU.add))

            sort_round(0, first=True)
            with v.Fori(1, ROUNDS - 1) as i:
                sort_round(i)
            sort_round(ROUNDS - 1, last=True)

            flag_column(0, 0, True)
            flag_column(1, 1, True)
            with v.Fori(1, NT // 2) as m:
                flag_column(2 * m, 0, False)
                flag_column(2 * m + 1, 1, False)

            v.wait_ge(s_xn, 32)
            then(nc.vector.tensor_tensor(xn[:], xn[:], b2b[:].unsqueeze(1).to_broadcast([P, NT, D]), ALU.add))
            v.wait_ge(s_flag, NT)
            for q in range(0, R, 512):
                n = min(512, R - q)
                last = nc.vector.tensor_scalar(keep[:, q:q + n], pF[:, q // 512, 0:n], 0.0, None, ALU.is_equal)
            last.then_inc(s_keepm, 1)
            v.wait_ge(s_end, 1)
            then(nc.vector.tensor_scalar(keepm[:], keep[:], 2.0, -1.0, ALU.mult, ALU.add))
            then(nc.vector.tensor_scalar(keepm[:], keepm[:], FLT_MAX, None, ALU.mult))
            first_row = sc[:, 0, :, :].rearrange("p a b -> p (a b)")[:, 0:R]
            then(nc.vector.scalar_tensor_tensor(out=first_row, in0=keep[:], scalar=float(R), in1=iota32[:],
                                                op0=ALU.mult, op1=ALU.add))
            then(nc.vector.tensor_reduce(t1[:, 0:1], first_row, AX.X, ALU.min))
            then(nc.vector.tensor_scalar(t1[:, 0:1], t1[:, 0:1], float(R), None, ALU.min))
            then(nc.vector.tensor_scalar(t1[:, 1:2], prowf[:], float(R - 1), -1.0 - SPARE, ALU.mult, ALU.add))
            then(nc.vector.tensor_tensor(t1[:, 1:2], t1[:, 1:2], t1[:, 0:1], ALU.add))
            then(nc.vector.tensor_scalar(t1[:, 2:3], t1[:, 0:1], 0.0, None, ALU.is_gt))
            then(nc.vector.tensor_tensor(t1[:, 1:2], t1[:, 1:2], t1[:, 2:3], ALU.mult))
            then(nc.vector.tensor_scalar(t1[:, 3:4], prowf[:], float(SPARE), None, ALU.add))
            then(nc.vector.tensor_tensor(t1[:, 1:2], t1[:, 1:2], t1[:, 3:4], ALU.add))
            nc.vector.tensor_copy(fixi[:], t1[:, 1:2]).then_inc(s_fi, 1)
            then(nc.vector.tensor_scalar(t1[:, 4:5], t1[:, 0:1], float(R), None, ALU.is_ge))
            then(nc.vector.tensor_scalar(t1[:, 5:6], t1[:, 4:5], 2.0, -1.0, ALU.mult, ALU.add))
            then(nc.vector.tensor_scalar(t1[:, 5:6], t1[:, 5:6], FLT_MAX, None, ALU.mult))
            then(nc.vector.tensor_copy(nf[:, 0:F], t1[:, 4:5].to_broadcast([P, F])))
            then(nc.vector.tensor_copy(nf[:, F:2 * F], t1[:, 5:6].to_broadcast([P, F])))

            def scan_chunk(k, b, first=False):
                v.wait_ge(s_xs[b], 16 * first_or(k, b))
                if not first:
                    v.wait_ge(s_sc, k)
                if not (isinstance(k, int) and k < 2):
                    v.wait_ge(s_so[b], 16 * (first_or(k, b) - 1))
                for f in range(F):
                    nc.vector.tensor_tensor_scan(
                        sc[:, b, :, f], keep[:, bass.ds(k * CH, CH)], xs[:, b, :, f],
                        0.0 if first else sc[:, 1 - b, CH - 1, f:f + 1], ALU.mult, ALU.add)
                    last = nc.vector.tensor_tensor_scan(
                        sc[:, b, :, F + f], keepm[:, bass.ds(k * CH, CH)], xs[:, b, :, f],
                        -FLT_MAX if first else sc[:, 1 - b, CH - 1, F + f:F + f + 1], ALU.min, ALU.max)
                last.then_inc(s_sc, 1)

            halves = {}

            def first_or(k, b):
                return halves["n"]

            halves["n"] = 1
            scan_chunk(0, 0, True)
            scan_chunk(1, 1)
            with v.Fori(1, NCH // 2) as m:
                halves["n"] = m + 1
                scan_chunk(2 * m, 0)
                scan_chunk(2 * m + 1, 1)
            halves["n"] = NCH // 2 + 1
            scan_chunk(NCH - 1, 0)

            v.wait_ge(s_sc, NCH)
            nc.vector.tensor_copy(carry[:], sc[:, 0, CH - 1, :]).then_inc(s_nf, 1)
            v.wait_ge(s_trT, 1)
            then(nc.vector.tensor_copy(tailT[:], pE[0][0:2 * F, 0, :]))
            then(nc.vector.tensor_copy(nfT[:], pE[0][0:2 * F, 1, :]))
            then(nc.vector.memset(chain[:, 0:1], 0.0))
            then(nc.vector.tensor_tensor_scan(chain[0:F, 1:P + 1], nfT[0:F, :], tailT[0:F, :], 0.0,
                                              ALU.mult, ALU.add))
            nc.vector.tensor_tensor_scan(chain[F:2 * F, 1:P + 1], nfT[F:2 * F, :], tailT[F:2 * F, :], -FLT_MAX,
                                         ALU.min, ALU.max).then_inc(s_ch, 1)
            v.wait_ge(s_fg, 16)
            v.wait_ge(s_cT, 1)
            nc.vector.tensor_tensor(fixo[:, 0:F], fixg[:, 0:F], pE[0][:, 0, 0:F], ALU.add)
            nc.vector.tensor_tensor(fixo[:, F:2 * F], fixg[:, F:2 * F], pE[0][:, 0, F:2 * F], ALU.max).then_inc(s_fo, 1)

            def numbers(q, b):
                nc.vector.tensor_copy(gi[:, b, :], endi[:, bass.ds(q * G, G)]).then_inc(s_gi, 1)

            def node_group(q, b, m, more):
                v.wait_ge(s_g[b], 16 * G * (m + 1))
                if more:
                    numbers(q + 2, b)
                nc.vector.tensor_tensor(
                    h[:, b, :, 2 * F:3 * F], h[:, b, :, 0:F],
                    rcnt[:, bass.ds(q * G, G)].unsqueeze(2).to_broadcast([P, G, F]), ALU.mult).then_inc(s_mean, 1)
                v.wait_ge(s_l2, q + 1)
                if not (isinstance(m, int) and m == 0):
                    v.wait_ge(s_out[b], 16 * m)
                nc.vector.tensor_tensor(y[:, b, :, :], pC[:, 0:G * D].rearrange("p (g d) -> p g d", g=G),
                                        xn[:, bass.ds(q * G, G), :], ALU.add).then_inc(s_y, 1)
                v.wait_ge(s_y, q + 1)
                for k in range(G):
                    last = nc.vector.bn_stats(st[:, b, k, :], y[:, b, k, :])
                last.then_inc(s_st, 1)
                v.wait_ge(s_st, q + 1)
                v.nop(nofuse=True)
                for k in range(G):
                    last = nc.vector.bn_aggr(mv[:, b, k, :], st[:, b, k, :])
                last.then_inc(s_mv, 1)
                v.wait_ge(s_mv, q + 1)
                nc.vector.tensor_scalar(rs[:, b, :], mv[:, b, :, 1], 1e-5, None, ALU.add).then_inc(s_ve, 1)
                v.wait_ge(s_sd, q + 1)
                nc.vector.reciprocal(rs[:, b, :], sd[:, b, :]).then_inc(s_rs, 1)
                v.wait_ge(s_rs, q + 1)
                for k in range(G):
                    last = nc.vector.tensor_scalar(y[:, b, k, :], y[:, b, k, :], mv[:, b, k, 0:1],
                                                   rs[:, b, k:k + 1], ALU.subtract, ALU.mult)
                last.then_inc(s_yn, 1)

            numbers(0, 0)
            numbers(1, 1)
            node_group(0, 0, 0, True)
            node_group(1, 1, 0, True)
            with v.Fori(1, GROUPS // 2 - 1) as m:
                node_group(2 * m, 0, m, True)
                node_group(2 * m + 1, 1, m, True)
            node_group(GROUPS - 2, 0, GROUPS // 2 - 1, False)
            node_group(GROUPS - 1, 1, GROUPS // 2 - 1, False)

        @block.tensor
        def _(t):
            mm = nc.tensor.matmul
            t.wait_ge(s_const, 9)
            t.wait_ge(s_castc, 4)
            mm(C, idf[:], zeros[:, 0:NT], start=True, stop=True)

            def count_round(i):
                for j in range(J):
                    t.wait_ge(s_oh1, J * i + j + 1)
                    for k in range(K):
                        last = mm(C, oh_lo[:, j, k, :], oh_hi[:, j, k, :], start=False, stop=True,
                                  skip_group_check=True)
                    last.then_inc(s_cnt, 1)

            with t.Fori(0, ROUNDS) as i:
                count_round(i)
            t.wait_ge(s_tot, 1)
            mm(pG[:, 0, 0:1], before[:], incl[:, NT - 1:NT], start=True, stop=True).then_inc(s_off, 1)
            t.wait_ge(s_start, 1)
            mm(C, idf[:], start[:], start=True, stop=True).then_inc(s_C, 1)

            def transposes(s, j, first):
                t.wait_ge(s_oh, s + 1)
                if not first:
                    t.wait_ge(s_loTf, s - 1)
                for k in range(K):
                    last = nc.tensor.transpose(pT[j % 2][:, k, :], oh_lo[:, j, k, :], idb[:])
                last.then_inc(s_T, 1)

            def matches(s, j, first):
                t.wait_ge(s_loT, s + 1)
                if not first:
                    t.wait_ge(s_earl, s - 1)
                mm(pE[j % 2], idb[:], late[:], start=True, stop=True)
                for k in range(K):
                    last = mm(pE[j % 2][:, k, :], loT[:, j % 2, k, :], loT[:, j % 2, k, :], start=False, stop=True,
                              skip_group_check=True)
                last.then_inc(s_eq, 1)

            def places(s, j, k, first):
                n = K * s + k
                if k == 0:
                    t.wait_ge(s_loTf, s + 1)
                    t.wait_ge(s_earl, s + 1)
                t.wait_ge(s_tab, n + 1)
                if not (first and k < 2):
                    t.wait_ge(s_pick, n - 1)
                row = pG[:, k % 2, 0:NT]
                mm(row, loTf[:, j % 2, k, :], table[:, k % 2, :], start=True, stop=False)
                mm(row, earlier[:, j % 2, k, :], oh_hi[:, j, k, :], start=False, stop=True).then_inc(s_G, 1)
                mm(C, oh_lo[:, j, k, :], oh_hi[:, j, k, :], start=False, stop=True,
                   skip_group_check=True).then_inc(s_C, 1)

            def sort_round(i, first=False, last=False):
                for j in range(J):
                    s = J * i + j
                    more = not (last and j == J - 1)
                    if more:
                        transposes(s + 1, (j + 1) % J, first and j == 0)
                    places(s, j, 0, first and j == 0)
                    places(s, j, 1, first and j == 0)
                    if more:
                        matches(s + 1, (j + 1) % J, first and j == 0)
                    places(s, j, 2, first and j == 0)
                    places(s, j, 3, first and j == 0)

            transposes(0, 0, True)
            matches(0, 0, True)
            sort_round(0, first=True)
            with t.Fori(1, ROUNDS - 1) as i:
                sort_round(i)
            sort_round(ROUNDS - 1, last=True)

            def flags(c, b, start):
                t.wait_ge(s_ohr, c + 1)
                for q in range(0, R, 512):
                    n = min(512, R - q)
                    last = mm(pF[:, q // 512, 0:n], ohq[:, b, :], ohr[:, b, q:q + n], start=start, stop=True,
                              skip_group_check=True)
                last.then_inc(s_flag, 1)

            flags(0, 0, True)
            flags(1, 1, False)
            with t.Fori(1, NT // 2) as m:
                flags(2 * m, 0, False)
                flags(2 * m + 1, 1, False)

            t.wait_ge(s_nf, 1)
            nc.tensor.transpose(pE[0][0:2 * F, 0, :], carry[:], idf[:])
            nc.tensor.transpose(pE[0][0:2 * F, 1, :], nf[:], idf[:]).then_inc(s_trT, 1)
            t.wait_ge(s_ch, 1)
            nc.tensor.transpose(pE[0][:, 0, 0:2 * F], chain[:, 0:P], idf[0:2 * F, 0:2 * F]).then_inc(s_cT, 1)
            t.wait_ge(s_fo, 1)

            def node_group(q, b, first):
                t.wait_ge(s_mean, q + 1)
                if not first:
                    t.wait_ge(s_hTc, q)
                for k in range(G):
                    last = nc.tensor.transpose(pF[0:3 * F, k // 4, (k % 4) * P:(k % 4 + 1) * P], h[:, b, k, :], idf[:])
                last.then_inc(s_hT, 1)
                t.wait_ge(s_hTc, q + 1)
                if not first:
                    t.wait_ge(s_r1, q)
                mm(pF[:, 2, :], w1[:], hT[:, 0:4, :], start=True, stop=True)
                mm(pF[:, 3, 0:(G - 4) * P], w1[:], hT[:, 4:G, :], start=True, stop=True).then_inc(s_l1, 1)
                t.wait_ge(s_r1, q + 1)
                if not first:
                    t.wait_ge(s_y, q)
                for k in range(G):
                    last = mm(pC[:, k * D:(k + 1) * D], r1[:, k, :], w2[:], start=True, stop=True)
                last.then_inc(s_l2, 1)

            node_group(0, 0, True)
            node_group(1, 1, False)
            with t.Fori(1, GROUPS // 2) as m:
                node_group(2 * m, 0, False)
                node_group(2 * m + 1, 1, False)

        @block.scalar
        def _(a):
            act = nc.scalar.activation

            def copy_T(s, j, kind):
                t_, done = (loT, s_loT) if kind == 0 else (loTf, s_loTf)
                a.wait_ge(s_T, s + 1)
                act(t_[:, j % 2, :, :], pT[j % 2], ACT.Copy).then_inc(done, 1)

            def relu_matches(s, j):
                a.wait_ge(s_eq, s + 1)
                act(earlier[:, j % 2, :, :], pE[j % 2], ACT.Relu).then_inc(s_earl, 1)

            def copy_table(n, k):
                a.wait_ge(s_C, n + 1)
                act(table[:, k % 2, :], C, ACT.Copy).then_inc(s_tab, 1)

            def sort_round(i, last=False):
                for j in range(J):
                    s = J * i + j
                    more = not (last and j == J - 1)
                    if more:
                        copy_T(s + 1, (j + 1) % J, 0)
                    copy_table(K * s + 1, 1)
                    if more:
                        copy_T(s + 1, (j + 1) % J, 1)
                    copy_table(K * s + 2, 2)
                    if more:
                        relu_matches(s + 1, (j + 1) % J)
                    copy_table(K * s + 3, 3)
                    if more:
                        copy_table(K * s + 4, 0)

            copy_T(0, 0, 0)
            copy_T(0, 0, 1)
            relu_matches(0, 0)
            copy_table(0, 0)
            with a.Fori(0, ROUNDS - 1) as i:
                sort_round(i)
            sort_round(ROUNDS - 1, last=True)

            def node_group(q, b, first):
                a.wait_ge(s_hT, q + 1)
                if not first:
                    a.wait_ge(s_l1, q)
                act(hT[:, 0:4, :].rearrange("p a b -> p (a b)"), pF[0:3 * F, 0, :], ACT.Copy)
                act(hT[:, 4:G, :].rearrange("p a b -> p (a b)"), pF[0:3 * F, 1, 0:(G - 4) * P],
                    ACT.Copy).then_inc(s_hTc, 1)
                a.wait_ge(s_l1, q + 1)
                if not first:
                    a.wait_ge(s_l2, q)
                act(r1[:, 0:4, :].rearrange("p a b -> p (a b)"), pF[:, 2, :], ACT.Relu, bias=bias1[:, 0:1])
                act(r1[:, 4:G, :].rearrange("p a b -> p (a b)"), pF[:, 3, 0:(G - 4) * P], ACT.Relu,
                    bias=bias1[:, 0:1]).then_inc(s_r1, 1)
                a.wait_ge(s_ve, q + 1)
                act(sd[:, b, :], rs[:, b, :], ACT.Sqrt).then_inc(s_sd, 1)

            node_group(0, 0, True)
            node_group(1, 1, False)
            with a.Fori(1, GROUPS // 2) as m:
                node_group(2 * m, 0, False)
                node_group(2 * m + 1, 1, False)


_INS = {"x": "x", "src": "src", "edge": "edge_attr_32", "u": "L0_gnn_u", "W1": "L0_gnn_W1", "b1": "L0_gnn_b1",
        "W2": "L0_gnn_W2", "b2": "L0_gnn_b2"}


def kernel(**inputs):
    import numpy as np
    import concourse.bacc as bacc
    from concourse.bass_utils import run_bass_kernel_spmd

    nc = bacc.Bacc("TRN2", target_bir_lowering=False, num_devices=1)
    arrays, args = {}, {}
    for arg, name in _INS.items():
        a = np.ascontiguousarray(inputs[name])
        arrays[f"in_{name}"] = a
        args[arg] = nc.dram_tensor(f"in_{name}", a.shape, mybir.dt.from_np(a.dtype), kind="ExternalInput").ap()
    shape = tuple(inputs["x"].shape)
    out = nc.dram_tensor("out_0", shape, mybir.dt.float32, kind="ExternalOutput").ap()
    gnn_kernel(nc, out=out, **args)
    r = run_bass_kernel_spmd(nc, [arrays], core_ids=[0])
    return r.results[0]["out_0"]
```

```python
import concourse.bass as bass
from concourse import mybir
from contextlib import ExitStack

P = 128
FLT_MAX = 3.4028234663852886e38


def gnn_kernel(nc, x, src, edge, u, W1, b1, W2, b2, out):
    f32, bf16 = mybir.dt.float32, mybir.dt.bfloat16
    i32, i16 = mybir.dt.int32, mybir.dt.int16
    ALU = mybir.AluOpType
    ACT = mybir.ActivationFunctionType
    AX = mybir.AxisListType

    N, D = x.shape
    E, F = edge.shape
    H = W1.shape[1]
    NT = -(-N // P)
    NLAST = N - (NT - 1) * P
    ET = E // P
    EREST = E - ET * P
    K = 4
    STEPS = -(-(ET + 1) // K)
    J = 4
    ROUNDS = STEPS // J
    COLS = STEPS * K
    assert ROUNDS * J == STEPS and (STEPS - 1) * K == ET
    NOHI = NT
    R = COLS
    ROWS = P * R
    SPARE = ROWS
    ZROW = ROWS + P
    NQ = 4
    RQ = R // NQ
    QR = -(-(NT + 1) // J)
    NC = QR * J
    assert 1 + NQ * QR <= ROUNDS - 1 and RQ <= 512
    CH = 128
    NCH = R // CH
    G = 7
    GROUPS = NT // G
    assert GROUPS * G == NT and NCH * CH == R and NCH % 2 and GROUPS % 2 == 0
    assert EREST <= P and ET % K == 0

    rows_dram = nc.dram_tensor("sorted_rows", [ROWS, F], f32, kind="Internal").ap()
    scan_dram = nc.dram_tensor("scanned_rows", [ROWS + 2 * P, 2 * F], f32, kind="Internal").ap()

    ctx = ExitStack()
    with ctx:
        def sb(name, shape, dt):
            return ctx.enter_context(nc.sbuf_tensor(name, shape, dt))

        def pb(name, shape, dt):
            return ctx.enter_context(nc.psum_tensor(name, shape, dt))

        def sem(name):
            return ctx.enter_context(nc.semaphore(name))

        idf = sb("idf", [P, P], f32)
        idb = sb("idb", [P, P], bf16)
        iota32 = sb("iota32", [P, R], i32)
        iota16 = sb("iota16", [P, R], i16)
        iota_b = sb("iota_b", [P, P], bf16)
        iotak32 = sb("iotak32", [P, P, K], i32)
        iotak = sb("iotak", [P, P, K], bf16)
        before = sb("before", [P, P], f32)
        late = sb("late", [P, K, P], bf16)
        prow = sb("prow", [P, 1], i32)
        prowf = sb("prowf", [P, 1], f32)
        zeros = sb("zeros", [P, P], f32)
        w1 = sb("w1", [3 * F, H], f32)
        w1u = sb("w1u", [P, 1], f32)
        ucol = sb("ucol", [P, 1], f32)
        b1c = sb("b1c", [P, 1], f32)
        bias1 = sb("bias1", [P, 1], f32)
        w2 = sb("w2", [H, D], f32)
        b2b = sb("b2b", [P, D], f32)
        srck = sb("srck", [P, COLS], i32)
        ki = sb("ki", [P, COLS], i32)
        keys = sb("keys", [P, 2, COLS], bf16)
        oh_lo = sb("oh_lo", [P, J, P, K], bf16)
        oh_hi = sb("oh_hi", [P, J, NT, K], bf16)
        loT = sb("loT", [P, 2, K, P], bf16)
        loTf = sb("loTf", [P, 2, K, P], f32)
        earlier = sb("earlier", [P, 2, K, P], bf16)
        table = sb("table", [P, 2, NT], f32)
        picked = sb("picked", [P, K, NT], f32)
        posf = sb("posf", [P, 2, K], f32)
        pos = sb("pos", [P, J, K], i32)
        feat = sb("feat", [P, J, K, F], f32)
        cnt = sb("cnt", [P, NT], f32)
        incl = sb("incl", [P, NT], f32)
        start = sb("start", [P, NT], f32)
        quo = sb("quo", [P, NT], f32)
        rem = sb("rem", [P, NT], f32)
        tmpn = sb("tmpn", [P, NT], f32)
        rcnt = sb("rcnt", [P, NT], f32)
        endf = sb("endf", [P, NT], f32)
        endi = sb("endi", [P, NT], i32)
        off = sb("off", [P, 1], f32)
        first_q = sb("first_q", [P, NC], f32)
        first_r = sb("first_r", [P, NQ, NC], f32)
        zb = sb("zb", [P, RQ], bf16)
        ohq = sb("ohq", [P, 2, P], bf16)
        ohr = sb("ohr", [P, 2, RQ], bf16)
        keep = sb("keep", [P, R], f32)
        keepm = sb("keepm", [P, R], f32)
        xs = sb("xs", [P, 2, CH, F], f32)
        sc = sb("sc", [P, 2, CH, 2 * F], f32)
        t1 = sb("t1", [P, 8], f32)
        fixi = sb("fixi", [P, 1], i32)
        nf = sb("nf", [P, 2 * F], f32)
        tailT = sb("tailT", [2 * F, P], f32)
        nfT = sb("nfT", [2 * F, P], f32)
        chain = sb("chain", [2 * F, P + 1], f32)
        carry = sb("carry", [P, 2 * F], f32)
        fixg = sb("fixg", [P, 2 * F], f32)
        fixo = sb("fixo", [P, 2 * F], f32)
        xn = sb("xn", [P, NT, D], f32)
        gi = sb("gi", [P, 2, G], i32)
        flat = xs[:].rearrange("p a b c -> p (a b c)")
        h = flat[:, 0:2 * G * 3 * F].rearrange("p (a g f) -> p a g f", a=2, g=G)
        y = flat[:, 2048:2048 + 2 * G * D].rearrange("p (a g f) -> p a g f", a=2, g=G)
        hT = flat[0:3 * F, 4096:4096 + G * P].rearrange("p (g n) -> p g n", g=G)
        r1 = flat[:, 6144:6144 + G * P].rearrange("p (g n) -> p g n", g=G)
        assert 2 * G * 3 * F <= 2048 and 2 * G * D <= 2048 and G * P <= 2048
        st = sb("st", [P, 2, G, 6], f32)
        mv = sb("mv", [P, 2, G, 2], f32)
        rs = sb("rs", [P, 2, G], f32)
        sd = sb("sd", [P, 2, G], f32)

        banks = pb("banks", [P, 8, 512], f32)
        pC = banks[:, 0, :]
        C = pC[:, 0:NT]
        pG = banks[:, 1:3, :]
        pE = [banks[:, b, :].rearrange("p (k n) -> p k n", k=K) for b in (3, 7)]
        pT = [banks[:, b, :].bitcast(bf16)[:, 0:K * P].rearrange("p (k n) -> p k n", k=K) for b in (4, 5)]
        pQ = banks[:, 6, 0:RQ]
        pF = banks[:, 4:8, :]

        s_const = sem("s_const")
        s_castc = sem("s_castc")
        s_src = sem("s_src")
        s_fill = sem("s_fill")
        s_w = sem("s_w")
        s_xn = sem("s_xn")
        s_xz = sem("s_xz")
        s_init = sem("s_init")
        s_keys = sem("s_keys")
        s_oh1 = sem("s_oh1")
        s_cnt = sem("s_cnt")
        s_tot = sem("s_tot")
        s_off = sem("s_off")
        s_start = sem("s_start")
        s_oh = sem("s_oh")
        s_T = sem("s_T")
        s_loT = sem("s_loT")
        s_loTf = sem("s_loTf")
        s_eq = sem("s_eq")
        s_earl = sem("s_earl")
        s_C = sem("s_C")
        s_tab = sem("s_tab")
        s_G = sem("s_G")
        s_pick = sem("s_pick")
        s_pos = sem("s_pos")
        s_feat = [sem(f"s_feat{j}") for j in range(J)]
        s_scat = [sem(f"s_scat{j}") for j in range(J)]
        s_ohr = sem("s_ohr")
        s_flag = sem("s_flag")
        s_keep = sem("s_keep")
        s_xs = [sem(f"s_xs{b}") for b in range(2)]
        s_sc = sem("s_sc")
        s_so = [sem(f"s_so{b}") for b in range(2)]
        s_nf = sem("s_nf")
        s_trT = sem("s_trT")
        s_ch = sem("s_ch")
        s_cT = sem("s_cT")
        s_fi = sem("s_fi")
        s_fg = sem("s_fg")
        s_fo = sem("s_fo")
        s_fs = sem("s_fs")
        s_v = sem("s_v")
        s_gi = sem("s_gi")
        s_g = [sem(f"s_g{b}") for b in range(2)]
        s_mean = sem("s_mean")
        s_hT = sem("s_hT")
        s_hTc = sem("s_hTc")
        s_l1 = sem("s_l1")
        s_r1 = sem("s_r1")
        s_l2 = sem("s_l2")
        s_y = sem("s_y")
        s_st = sem("s_st")
        s_mv = sem("s_mv")
        s_ve = sem("s_ve")
        s_sd = sem("s_sd")
        s_rs = sem("s_rs")
        s_yn = sem("s_yn")
        s_out = [sem(f"s_out{b}") for b in range(2)]

        block = ctx.enter_context(nc.Block())

        edge_t = edge[0:ET * P, :].rearrange("(p t) f -> p t f", t=ET)
        rows_p = rows_dram.rearrange("(p r) f -> p r f", r=R)
        scan_p = scan_dram[0:ROWS, :].rearrange("(p r) f -> p r f", r=R)
        x_t = x[0:(NT - 1) * P, :].rearrange("(t p) d -> p t d", p=P)
        out_t = out[0:(NT - 1) * P, :].rearrange("(t p) d -> p t d", p=P)

        @block.sync
        def _(sp):
            sp.dma_start(srck[:, 0:ET], src[0:ET * P].rearrange("(p t) -> p t", t=ET)).then_inc(s_src, 16)
            sp.wait_ge(s_fill, 1)
            sp.dma_start(srck[0:EREST, ET:ET + 1],
                         src[ET * P:E].rearrange("(p o) -> p o", o=1)).then_inc(s_src, 16)

            def load_rows(i, j):
                if not (isinstance(i, int) and i == 0):
                    sp.wait_ge(s_scat[j], 16 * K * i)
                sp.dma_start(feat[:, j, :, :],
                             edge_t[:, bass.ds(K * (J * i + j), K), :]).then_inc(s_feat[j], 16)

            for j in range(J):
                load_rows(0, j)
            sp.dma_start(w1[:], W1[0:3 * F, :]).then_inc(s_w, 16)
            sp.dma_start(w1u[:], W1[3 * F:3 * F + 1, :].rearrange("o h -> h o")).then_inc(s_w, 16)
            sp.dma_start(ucol[:], u[0:1, 0:1].to_broadcast([P, 1])).then_inc(s_w, 16)
            sp.dma_start(b1c[:], b1.rearrange("(h o) -> h o", o=1)).then_inc(s_w, 16)
            sp.dma_start(w2[:], W2).then_inc(s_w, 16)
            sp.dma_start(b2b[:], b2.rearrange("(o d) -> o d", o=1).to_broadcast([P, D])).then_inc(s_w, 16)
            sp.wait_ge(s_const, 1)
            pad = ROWS - E
            part = pad // 4
            sp.dma_start(rows_dram[E:ROWS, :].rearrange("(p k) f -> p (k f)", k=4),
                         zeros[0:part, 0:4 * F]).then_inc(s_init, 16)
            sp.dma_start(scan_dram[ROWS:ROWS + 2 * P, :].rearrange("(p k) f -> p (k f)", k=2),
                         zeros[:, 0:4 * F]).then_inc(s_init, 16)
            sp.wait_ge(s_xz, 1)
            sp.dma_start(xn[:, 0:NT - 1, :], x_t).then_inc(s_xn, 16)
            sp.dma_start(xn[0:NLAST, NT - 1, :], x[(NT - 1) * P:N, :]).then_inc(s_xn, 16)
            with sp.Fori(1, ROUNDS - 1) as i:
                for j in range(J):
                    load_rows(i, j)
            for j in range(J - 1):
                load_rows(ROUNDS - 1, j)
            j = J - 1
            sp.wait_ge(s_scat[j], 16 * K * (ROUNDS - 1))
            sp.dma_start(feat[0:EREST, j, 0, :], edge[ET * P:E, :]).then_inc(s_feat[j], 16)

            sp.wait_ge(s_init, 32)
            for j in range(J):
                sp.wait_ge(s_scat[j], 16 * K * ROUNDS if j < J - 1 else 16 * (K * (ROUNDS - 1) + 1))

            def load_chunk(k, b):
                sp.dma_start(xs[:, b, :, :], rows_p[:, bass.ds(k * CH, CH), :]).then_inc(s_xs[b], 16)

            def store_chunk(k, b):
                sp.wait_ge(s_sc, k + 1)
                sp.dma_start(scan_p[:, bass.ds(k * CH, CH), :], sc[:, b, :, :]).then_inc(s_so[b], 16)

            load_chunk(0, 0)
            load_chunk(1, 1)
            store_chunk(0, 0)
            load_chunk(2, 0)
            with sp.Fori(0, NCH // 2 - 1) as m:
                store_chunk(2 * m + 1, 1)
                load_chunk(2 * m + 3, 1)
                store_chunk(2 * m + 2, 0)
                load_chunk(2 * m + 4, 0)
            store_chunk(NCH - 2, 1)
            store_chunk(NCH - 1, 0)

            def store_group(g, b):
                sp.wait_ge(s_yn, g + 1)
                sp.dma_start(out_t[:, bass.ds(g * G, G), :], y[:, b, :, :]).then_inc(s_out[b], 16)

            with sp.Fori(0, GROUPS // 2 - 1) as m:
                store_group(2 * m, 0)
                store_group(2 * m + 1, 1)
            store_group(GROUPS - 2, 0)
            sp.wait_ge(s_yn, GROUPS)
            sp.dma_start(out_t[:, NT - G:NT - 1, :], y[:, 1, 0:G - 1, :]).then_inc(s_out[1], 16)
            sp.dma_start(out[(NT - 1) * P:N, :], y[0:NLAST, 1, G - 1, :]).then_inc(s_out[1], 16)
            sp.wait_ge(s_out[0], 16 * (GROUPS // 2))
            sp.wait_ge(s_out[1], 16 * (GROUPS // 2 + 1))

        @block.gpsimd
        def _(g):
            nc.gpsimd.memset(zeros[:], 0.0).then_inc(s_const, 1)
            g.iota(iota32[:], pattern=[[1, R]], base=0, channel_multiplier=0).then_inc(s_const, 1)
            g.iota(iotak32[:], pattern=[[1, P], [0, K]], base=0, channel_multiplier=0).then_inc(s_const, 1)
            g.iota(prow[:], pattern=[[1, 1]], base=0, channel_multiplier=1).then_inc(s_const, 1)
            nc.gpsimd.memset(idf[:], 0.0).then_inc(s_const, 1)
            nc.gpsimd.memset(before[:], 1.0).then_inc(s_const, 1)
            nc.gpsimd.memset(late[:], -1.0).then_inc(s_const, 1)
            nc.gpsimd.memset(zb[:], 0.0).then_inc(s_const, 1)
            g.wait_ge(s_const, 8)
            g.affine_select(out=idf[:], in_=idf[:], compare_op=ALU.not_equal, fill=1.0, base=0,
                            pattern=[[-1, P]], channel_multiplier=1).then_inc(s_const, 1)
            g.affine_select(out=before[:], in_=before[:], compare_op=ALU.is_gt, fill=0.0, base=0,
                            pattern=[[1, P]], channel_multiplier=-1).then_inc(s_const, 1)
            g.affine_select(out=late[:], in_=late[:], compare_op=ALU.is_ge, fill=0.0, base=0,
                            pattern=[[0, K], [-1, P]], channel_multiplier=1).then_inc(s_const, 1)
            nc.gpsimd.memset(xn[:, NT - 1, :], 0.0).then_inc(s_xz, 1)

            def scatter(i, j, tiles, parts):
                g.wait_ge(s_feat[j], 16 * (i + 1))
                g.wait_ge(s_pos, J * i + j + 1)
                g.nop(nofuse=True)
                for k in range(tiles):
                    g.indirect_dma_start(rows_dram, bass.IndirectOffsetOnAxis(pos[0:parts, j, k:k + 1], 0),
                                         feat[0:parts, j, k, :], None).then_inc(s_scat[j], 16)

            with g.Fori(0, ROUNDS - 1) as i:
                for j in range(J):
                    scatter(i, j, K, P)
            for j in range(J - 1):
                scatter(ROUNDS - 1, j, K, P)
            scatter(ROUNDS - 1, J - 1, 1, EREST)

            g.wait_ge(s_fi, 1)
            g.wait_ge(s_so[0], 16 * (NCH // 2 + 1))
            g.wait_ge(s_so[1], 16 * (NCH // 2))
            g.indirect_dma_start(fixg[:], None, scan_dram, bass.IndirectOffsetOnAxis(fixi[:, 0:1], 0)).then_inc(s_fg, 16)
            g.wait_ge(s_fo, 1)
            g.indirect_dma_start(scan_dram, bass.IndirectOffsetOnAxis(fixi[:, 0:1], 0), fixo[:], None).then_inc(s_fs, 16)
            g.wait_ge(s_fs, 16)

            def gather(q, b):
                if not (isinstance(q, int) and q < 2):
                    g.wait_ge(s_hT, q - 1)
                g.wait_ge(s_gi, q + 1)
                g.nop(nofuse=True)
                for k in range(G):
                    g.indirect_dma_start(h[:, b, k, 0:2 * F], None, scan_dram,
                                         bass.IndirectOffsetOnAxis(gi[:, b, k:k + 1], 0)).then_inc(s_g[b], 16)

            gather(0, 0)
            gather(1, 1)
            with g.Fori(1, GROUPS // 2) as m:
                gather(2 * m, 0)
                gather(2 * m + 1, 1)

        @block.vector
        def _(v):
            order = [0]

            def then(ins):
                order[0] += 1
                ins.then_inc(s_v, 1)
                v.wait_ge(s_v, order[0])

            nc.vector.memset(srck[:, ET:COLS], NOHI * P).then_inc(s_fill, 1)
            v.wait_ge(s_const, 11)
            nc.vector.tensor_copy(iota_b[:], iota32[:, 0:P]).then_inc(s_castc, 1)
            nc.vector.tensor_copy(iota16[:], iota32[:]).then_inc(s_castc, 1)
            nc.vector.tensor_copy(iotak[:], iotak32[:]).then_inc(s_castc, 1)
            nc.vector.tensor_copy(idb[:], idf[:]).then_inc(s_castc, 1)
            nc.vector.tensor_copy(prowf[:], prow[:]).then_inc(s_castc, 1)
            v.wait_ge(s_src, 32)
            then(nc.vector.tensor_single_scalar(ki[:], srck[:], P - 1, op=ALU.bitwise_and))
            nc.vector.tensor_copy(keys[:, 0, :], ki[:]).then_inc(s_keys, 1)
            v.wait_ge(s_keys, 1)
            then(nc.vector.tensor_single_scalar(ki[:], srck[:], 7, op=ALU.arith_shift_right))
            nc.vector.tensor_copy(keys[:, 1, :], ki[:]).then_inc(s_keys, 1)
            v.wait_ge(s_keys, 2)
            v.wait_ge(s_castc, 5)

            def one_hots(c, j, m, done):
                for kind, oh, width in ((0, oh_lo, P), (1, oh_hi, NT)):
                    part = keys[:, kind, bass.ds(c, m * K)].rearrange("p (m k) -> p m k", m=m).unsqueeze(2)
                    if m == 1:
                        last = nc.vector.tensor_tensor(oh[:, j, :, :], part[:, 0, :, :].to_broadcast([P, width, K]),
                                                       iotak[:, 0:width, :], ALU.is_equal)
                    else:
                        last = nc.vector.tensor_tensor(
                            oh[:, j:j + m, :, :], part.to_broadcast([P, m, width, K]),
                            iotak[:, 0:width, :].unsqueeze(1).to_broadcast([P, m, width, K]), ALU.is_equal)
                last.then_inc(done, 1)

            def count_round(i, first=False):
                for half in range(2):
                    if not first:
                        v.wait_ge(s_cnt, 2 * i + half - 1)
                    one_hots(J * K * i + 2 * K * half, 2 * half, 2, s_oh1)

            count_round(0, True)
            with v.Fori(1, ROUNDS) as i:
                count_round(i)

            v.wait_ge(s_cnt, STEPS // 2)
            then(nc.vector.tensor_copy(cnt[:], C))
            then(nc.vector.memset(tmpn[:], 1.0))
            nc.vector.tensor_tensor_scan(incl[:], tmpn[:], cnt[:], 0.0, ALU.mult, ALU.add).then_inc(s_tot, 1)
            v.wait_ge(s_off, 1)
            v.wait_ge(s_tot, 1)
            then(nc.vector.tensor_copy(off[:], pG[:, 0, 0:1]))
            then(nc.vector.tensor_tensor(start[:], incl[:], cnt[:], ALU.subtract))
            nc.vector.tensor_scalar(start[:], start[:], off[:, 0:1], None, ALU.add).then_inc(s_start, 1)
            v.wait_ge(s_start, 1)

            def prepare(s, j, i0):
                if not i0:
                    v.wait_ge(s_C, K * (s - J) + K + 1)
                    v.wait_ge(s_pick, K * (s - J) + K)
                one_hots(K * s, j, 1, s_oh)

            def pick(s, j, first):
                for k in range(K):
                    if not first:
                        v.wait_ge(s_pick, K * (s - 1) + k + 1)
                        if k == 0 and not (isinstance(s, int) and s < 2):
                            v.wait_ge(s_pos, s - 1)
                    v.wait_ge(s_G, K * s + k + 1)
                    nc.vector.scalar_tensor_tensor(
                        out=picked[:, k, :], in0=pG[:, k % 2, 0:NT], scalar=1.0, in1=oh_hi[:, j, :, k],
                        op0=ALU.mult, op1=ALU.mult, accum_out=posf[:, j % 2, k:k + 1]).then_inc(s_pick, 1)

            def to_int(s, j, i):
                v.wait_ge(s_pick, K * (s + 1))
                if not (isinstance(i, int) and i == 0):
                    v.wait_ge(s_scat[j], 16 * K * i)
                nc.vector.tensor_copy(pos[:, j, :], posf[:, j % 2, :]).then_inc(s_pos, 1)

            def flag_column(c, n, q, b):
                v.wait_ge(s_flag, n + 2 * q + 1)
                nc.vector.tensor_scalar(ohq[:, b, :], iota_b[:], first_q[:, bass.ds(c, 1)], None, ALU.is_equal)
                nc.vector.tensor_scalar(ohr[:, b, :], iota16[:, 0:RQ], flat_r[:, bass.ds(n, 1)], None,
                                        ALU.is_equal).then_inc(s_ohr, 1)

            flat_r = first_r[:].rearrange("p q c -> p (q c)")

            def sort_round(i, first=False, last=False, q=None, r=None):
                for j in range(J):
                    s = J * i + j
                    if not (last and j + 2 >= J):
                        prepare(s + 2, (j + 2) % J, first and j + 2 < J)
                    if r is not None:
                        flag_column(J * r + j, J * (i - 1) + j, q, j % 2)
                    pick(s, j, first and j == 0)
                    to_int(s, j, i)

            for s in range(2):
                prepare(s, s, True)
            then(nc.vector.tensor_scalar(quo[:], start[:], 1.0 / R, 0.5 / R - 0.5, ALU.mult, ALU.add))
            then(nc.vector.tensor_scalar(quo[:], quo[:], 12582912.0, 12582912.0, ALU.add, ALU.subtract))
            then(nc.vector.scalar_tensor_tensor(out=rem[:], in0=quo[:], scalar=-float(R), in1=start[:],
                                                op0=ALU.mult, op1=ALU.add))
            then(nc.vector.memset(first_q[:, NT:NC], -1.0))
            then(nc.vector.memset(first_r[:, 0, NT:NC], -1.0))
            then(nc.vector.memset(first_q[0:1, NT:NT + 1], float(E // R)))
            then(nc.vector.memset(first_r[0:1, 0, NT:NT + 1], float(E % R)))
            then(nc.vector.tensor_copy(first_q[:, 0:NT], quo[:]))
            then(nc.vector.tensor_copy(first_r[:, 0, 0:NT], rem[:]))
            for q in range(1, NQ):
                then(nc.vector.tensor_scalar(first_r[:, q, :], first_r[:, 0, :], -float(q * RQ), None, ALU.add))
            v.sem_inc(s_keep, 1)
            then(nc.vector.tensor_scalar(rcnt[:], cnt[:], 1.0, None, ALU.max))
            then(nc.vector.reciprocal(rcnt[:], rcnt[:]))
            then(nc.vector.scalar_tensor_tensor(out=endf[:], in0=cnt[:], scalar=-1.0 - ZROW, in1=start[:],
                                                op0=ALU.add, op1=ALU.add))
            then(nc.vector.tensor_scalar(tmpn[:], cnt[:], 0.0, None, ALU.is_gt))
            then(nc.vector.tensor_tensor(endf[:], endf[:], tmpn[:], ALU.mult))
            then(nc.vector.tensor_scalar(endf[:], endf[:], float(ZROW), None, ALU.add))
            then(nc.vector.tensor_copy(endi[:], endf[:]))
            v.wait_ge(s_w, 96)
            then(nc.vector.tensor_scalar(bias1[:], w1u[:], ucol[:, 0:1], b1c[:, 0:1], ALU.mult, ALU.add))

            sort_round(0, first=True)
            v.wait_ge(s_xn, 32)
            then(nc.vector.tensor_tensor(xn[:], xn[:], b2b[:].unsqueeze(1).to_broadcast([P, NT, D]), ALU.add))
            with v.Fori(0, NQ) as q:
                with v.Fori(0, QR) as r:
                    sort_round(QR * q + r + 1, q=q, r=r)
                v.wait_ge(s_flag, (NC + 2) * (q + 1))
                nc.vector.tensor_scalar(keep[:, bass.ds(RQ * q, RQ)], pQ, 0.0, None, ALU.is_equal).then_inc(s_keep, 1)
            with v.Fori(1 + NQ * QR, ROUNDS - 1) as i:
                sort_round(i)
            sort_round(ROUNDS - 1, last=True)

            v.wait_ge(s_keep, NQ + 1)
            then(nc.vector.tensor_scalar(keepm[:], keep[:], 2.0, -1.0, ALU.mult, ALU.add))
            then(nc.vector.tensor_scalar(keepm[:], keepm[:], FLT_MAX, None, ALU.mult))
            first_row = sc[:, 0, :, :].rearrange("p a b -> p (a b)")[:, 0:R]
            then(nc.vector.scalar_tensor_tensor(out=first_row, in0=keep[:], scalar=float(R), in1=iota32[:],
                                                op0=ALU.mult, op1=ALU.add))
            then(nc.vector.tensor_reduce(t1[:, 0:1], first_row, AX.X, ALU.min))
            then(nc.vector.tensor_scalar(t1[:, 0:1], t1[:, 0:1], float(R), None, ALU.min))
            then(nc.vector.tensor_scalar(t1[:, 1:2], prowf[:], float(R - 1), -1.0 - SPARE, ALU.mult, ALU.add))
            then(nc.vector.tensor_tensor(t1[:, 1:2], t1[:, 1:2], t1[:, 0:1], ALU.add))
            then(nc.vector.tensor_scalar(t1[:, 2:3], t1[:, 0:1], 0.0, None, ALU.is_gt))
            then(nc.vector.tensor_tensor(t1[:, 1:2], t1[:, 1:2], t1[:, 2:3], ALU.mult))
            then(nc.vector.tensor_scalar(t1[:, 3:4], prowf[:], float(SPARE), None, ALU.add))
            then(nc.vector.tensor_tensor(t1[:, 1:2], t1[:, 1:2], t1[:, 3:4], ALU.add))
            nc.vector.tensor_copy(fixi[:], t1[:, 1:2]).then_inc(s_fi, 1)
            then(nc.vector.tensor_scalar(t1[:, 4:5], t1[:, 0:1], float(R), None, ALU.is_ge))
            then(nc.vector.tensor_scalar(t1[:, 5:6], t1[:, 4:5], 2.0, -1.0, ALU.mult, ALU.add))
            then(nc.vector.tensor_scalar(t1[:, 5:6], t1[:, 5:6], FLT_MAX, None, ALU.mult))
            then(nc.vector.tensor_copy(nf[:, 0:F], t1[:, 4:5].to_broadcast([P, F])))
            then(nc.vector.tensor_copy(nf[:, F:2 * F], t1[:, 5:6].to_broadcast([P, F])))

            def scan_chunk(k, b, first=False):
                v.wait_ge(s_xs[b], 16 * first_or(k, b))
                if not first:
                    v.wait_ge(s_sc, k)
                if not (isinstance(k, int) and k < 2):
                    v.wait_ge(s_so[b], 16 * (first_or(k, b) - 1))
                for f in range(F):
                    nc.vector.tensor_tensor_scan(
                        sc[:, b, :, f], keep[:, bass.ds(k * CH, CH)], xs[:, b, :, f],
                        0.0 if first else sc[:, 1 - b, CH - 1, f:f + 1], ALU.mult, ALU.add)
                    last = nc.vector.tensor_tensor_scan(
                        sc[:, b, :, F + f], keepm[:, bass.ds(k * CH, CH)], xs[:, b, :, f],
                        -FLT_MAX if first else sc[:, 1 - b, CH - 1, F + f:F + f + 1], ALU.min, ALU.max)
                last.then_inc(s_sc, 1)

            halves = {}

            def first_or(k, b):
                return halves["n"]

            halves["n"] = 1
            scan_chunk(0, 0, True)
            scan_chunk(1, 1)
            with v.Fori(1, NCH // 2) as m:
                halves["n"] = m + 1
                scan_chunk(2 * m, 0)
                scan_chunk(2 * m + 1, 1)
            halves["n"] = NCH // 2 + 1
            scan_chunk(NCH - 1, 0)

            v.wait_ge(s_sc, NCH)
            nc.vector.tensor_copy(carry[:], sc[:, 0, CH - 1, :]).then_inc(s_nf, 1)
            v.wait_ge(s_trT, 1)
            then(nc.vector.tensor_copy(tailT[:], pE[0][0:2 * F, 0, :]))
            then(nc.vector.tensor_copy(nfT[:], pE[0][0:2 * F, 1, :]))
            then(nc.vector.memset(chain[:, 0:1], 0.0))
            then(nc.vector.tensor_tensor_scan(chain[0:F, 1:P + 1], nfT[0:F, :], tailT[0:F, :], 0.0,
                                              ALU.mult, ALU.add))
            nc.vector.tensor_tensor_scan(chain[F:2 * F, 1:P + 1], nfT[F:2 * F, :], tailT[F:2 * F, :], -FLT_MAX,
                                         ALU.min, ALU.max).then_inc(s_ch, 1)
            v.wait_ge(s_fg, 16)
            v.wait_ge(s_cT, 1)
            nc.vector.tensor_tensor(fixo[:, 0:F], fixg[:, 0:F], pE[0][:, 0, 0:F], ALU.add)
            nc.vector.tensor_tensor(fixo[:, F:2 * F], fixg[:, F:2 * F], pE[0][:, 0, F:2 * F], ALU.max).then_inc(s_fo, 1)

            def numbers(q, b):
                nc.vector.tensor_copy(gi[:, b, :], endi[:, bass.ds(q * G, G)]).then_inc(s_gi, 1)

            def means(q, b, m, more):
                v.wait_ge(s_g[b], 16 * G * (m + 1))
                if more:
                    numbers(q + 2, b)
                nc.vector.tensor_tensor(
                    h[:, b, :, 2 * F:3 * F], h[:, b, :, 0:F],
                    rcnt[:, bass.ds(q * G, G)].unsqueeze(2).to_broadcast([P, G, F]), ALU.mult).then_inc(s_mean, 1)

            def norms(q, b, m):
                v.wait_ge(s_l2, q + 1)
                if not (isinstance(m, int) and m == 0):
                    v.wait_ge(s_out[b], 16 * m)
                nc.vector.tensor_tensor(y[:, b, :, :], pC[:, 0:G * D].rearrange("p (g d) -> p g d", g=G),
                                        xn[:, bass.ds(q * G, G), :], ALU.add).then_inc(s_y, 1)
                v.wait_ge(s_y, q + 1)
                for k in range(G):
                    last = nc.vector.bn_stats(st[:, b, k, :], y[:, b, k, :])
                last.then_inc(s_st, 1)
                v.wait_ge(s_st, q + 1)
                v.nop(nofuse=True)
                for k in range(G):
                    last = nc.vector.bn_aggr(mv[:, b, k, :], st[:, b, k, :])
                last.then_inc(s_mv, 1)
                v.wait_ge(s_mv, q + 1)
                nc.vector.tensor_scalar(rs[:, b, :], mv[:, b, :, 1], 1e-5, None, ALU.add).then_inc(s_ve, 1)

            def finish(q, b):
                v.wait_ge(s_sd, q + 1)
                nc.vector.reciprocal(rs[:, b, :], sd[:, b, :]).then_inc(s_rs, 1)
                v.wait_ge(s_rs, q + 1)
                for k in range(G):
                    last = nc.vector.tensor_scalar(y[:, b, k, :], y[:, b, k, :], mv[:, b, k, 0:1],
                                                   rs[:, b, k:k + 1], ALU.subtract, ALU.mult)
                last.then_inc(s_yn, 1)

            def turn(q, b, m, more=True):
                means(q, b, m, more)
                norms(q - 1, 1 - b, m - (1 - b))
                finish(q - 2, b)

            last_m = GROUPS // 2 - 1
            numbers(0, 0)
            numbers(1, 1)
            means(0, 0, 0, True)
            means(1, 1, 0, True)
            norms(0, 0, 0)
            turn(2, 0, 1)
            turn(3, 1, 1)
            with v.Fori(2, last_m) as m:
                turn(2 * m, 0, m)
                turn(2 * m + 1, 1, m)
            turn(GROUPS - 2, 0, last_m, False)
            turn(GROUPS - 1, 1, last_m, False)
            norms(GROUPS - 1, 1, last_m)
            finish(GROUPS - 2, 0)
            finish(GROUPS - 1, 1)

        @block.tensor
        def _(t):
            mm = nc.tensor.matmul
            t.wait_ge(s_const, 11)
            t.wait_ge(s_castc, 5)
            mm(C, idf[:], zeros[:, 0:NT], start=True, stop=True)

            def count_round(i):
                for half in range(2):
                    t.wait_ge(s_oh1, 2 * i + half + 1)
                    for j in (2 * half, 2 * half + 1):
                        for k in range(K):
                            last = mm(C, oh_lo[:, j, :, k], oh_hi[:, j, :, k], start=False, stop=True,
                                      skip_group_check=True)
                    last.then_inc(s_cnt, 1)

            with t.Fori(0, ROUNDS) as i:
                count_round(i)
            t.wait_ge(s_tot, 1)
            mm(pG[:, 0, 0:1], before[:], incl[:, NT - 1:NT], start=True, stop=True).then_inc(s_off, 1)
            t.wait_ge(s_start, 1)
            mm(C, idf[:], start[:], start=True, stop=True).then_inc(s_C, 1)

            def transposes(s, j, first):
                t.wait_ge(s_oh, s + 1)
                if not first:
                    t.wait_ge(s_loTf, s - 1)
                for k in range(K):
                    last = nc.tensor.transpose(pT[j % 2][:, k, :], oh_lo[:, j, :, k], idb[:])
                last.then_inc(s_T, 1)

            def matches(s, j, first):
                t.wait_ge(s_loT, s + 1)
                if not first:
                    t.wait_ge(s_earl, s - 1)
                mm(pE[j % 2], idb[:], late[:], start=True, stop=True)
                for k in range(K):
                    last = mm(pE[j % 2][:, k, :], loT[:, j % 2, k, :], loT[:, j % 2, k, :], start=False, stop=True,
                              skip_group_check=True)
                last.then_inc(s_eq, 1)

            def places(s, j, k, first):
                n = K * s + k
                if k == 0:
                    t.wait_ge(s_loTf, s + 1)
                    t.wait_ge(s_earl, s + 1)
                t.wait_ge(s_tab, n + 1)
                mm(C, oh_lo[:, j, :, k], oh_hi[:, j, :, k], start=False, stop=True,
                   skip_group_check=True).then_inc(s_C, 1)
                if not (first and k < 2):
                    t.wait_ge(s_pick, n - 1)
                row = pG[:, k % 2, 0:NT]
                mm(row, loTf[:, j % 2, k, :], table[:, k % 2, :], start=True, stop=False)
                mm(row, earlier[:, j % 2, k, :], oh_hi[:, j, :, k], start=False, stop=True).then_inc(s_G, 1)

            def flags(n, b):
                t.wait_ge(s_ohr, n + 1)
                mm(pQ, ohq[:, b, :], ohr[:, b, :], start=False, stop=True, skip_group_check=True).then_inc(s_flag, 1)

            def sort_round(i, first=False, last=False, marks=False):
                for j in range(J):
                    s = J * i + j
                    more = not (last and j == J - 1)
                    if more:
                        transposes(s + 1, (j + 1) % J, first and j == 0)
                    places(s, j, 0, first and j == 0)
                    places(s, j, 1, first and j == 0)
                    if more:
                        matches(s + 1, (j + 1) % J, first and j == 0)
                    places(s, j, 2, first and j == 0)
                    places(s, j, 3, first and j == 0)
                    if marks:
                        flags(J * (i - 1) + j, j % 2)

            transposes(0, 0, True)
            matches(0, 0, True)
            sort_round(0, first=True)
            with t.Fori(0, NQ) as q:
                t.wait_ge(s_keep, q + 1)
                mm(pQ, zb[:, 0:P], zb[:], start=True, stop=True).then_inc(s_flag, 2)
                with t.Fori(0, QR) as r:
                    sort_round(QR * q + r + 1, marks=True)
            with t.Fori(1 + NQ * QR, ROUNDS - 1) as i:
                sort_round(i)
            sort_round(ROUNDS - 1, last=True)

            t.wait_ge(s_nf, 1)
            nc.tensor.transpose(pE[0][0:2 * F, 0, :], carry[:], idf[:])
            nc.tensor.transpose(pE[0][0:2 * F, 1, :], nf[:], idf[:]).then_inc(s_trT, 1)
            t.wait_ge(s_ch, 1)
            nc.tensor.transpose(pE[0][:, 0, 0:2 * F], chain[:, 0:P], idf[0:2 * F, 0:2 * F]).then_inc(s_cT, 1)
            t.wait_ge(s_fo, 1)

            def turn(q, b, first):
                t.wait_ge(s_mean, q + 1)
                if not first:
                    t.wait_ge(s_hTc, q)
                for k in range(G):
                    last = nc.tensor.transpose(pF[0:3 * F, k // 4, (k % 4) * P:(k % 4 + 1) * P], h[:, b, k, :], idf[:])
                last.then_inc(s_hT, 1)

            def layer1(q, first):
                t.wait_ge(s_hTc, q + 1)
                if not first:
                    t.wait_ge(s_r1, q)
                mm(pF[:, 2, :], w1[:], hT[:, 0:4, :], start=True, stop=True)
                mm(pF[:, 3, 0:(G - 4) * P], w1[:], hT[:, 4:G, :], start=True, stop=True).then_inc(s_l1, 1)

            def layer2(q, first):
                t.wait_ge(s_r1, q + 1)
                if not first:
                    t.wait_ge(s_y, q)
                for k in range(G):
                    last = mm(pC[:, k * D:(k + 1) * D], r1[:, k, :], w2[:], start=True, stop=True)
                last.then_inc(s_l2, 1)

            turn(0, 0, True)
            layer1(0, True)
            turn(1, 1, False)
            layer2(0, True)
            with t.Fori(0, GROUPS // 2 - 1) as m:
                layer1(2 * m + 1, False)
                turn(2 * m + 2, 0, False)
                layer2(2 * m + 1, False)
                layer1(2 * m + 2, False)
                turn(2 * m + 3, 1, False)
                layer2(2 * m + 2, False)
            layer1(GROUPS - 1, False)
            layer2(GROUPS - 1, False)

        @block.scalar
        def _(a):
            act = nc.scalar.activation

            def copy_T(s, j, kind):
                t_, done = (loT, s_loT) if kind == 0 else (loTf, s_loTf)
                a.wait_ge(s_T, s + 1)
                act(t_[:, j % 2, :, :], pT[j % 2], ACT.Copy).then_inc(done, 1)

            def relu_matches(s, j):
                a.wait_ge(s_eq, s + 1)
                act(earlier[:, j % 2, :, :], pE[j % 2], ACT.Relu).then_inc(s_earl, 1)

            def copy_table(n, k):
                a.wait_ge(s_C, n + 1)
                act(table[:, k % 2, :], C, ACT.Copy).then_inc(s_tab, 1)

            def sort_round(i, last=False):
                for j in range(J):
                    s = J * i + j
                    more = not (last and j == J - 1)
                    if more:
                        copy_T(s + 1, (j + 1) % J, 0)
                    copy_table(K * s + 1, 1)
                    if more:
                        copy_T(s + 1, (j + 1) % J, 1)
                    copy_table(K * s + 2, 2)
                    if more:
                        relu_matches(s + 1, (j + 1) % J)
                    copy_table(K * s + 3, 3)
                    if more:
                        copy_table(K * s + 4, 0)

            copy_T(0, 0, 0)
            copy_T(0, 0, 1)
            relu_matches(0, 0)
            copy_table(0, 0)
            with a.Fori(0, ROUNDS - 1) as i:
                sort_round(i)
            sort_round(ROUNDS - 1, last=True)

            def copy_h(q, first):
                a.wait_ge(s_hT, q + 1)
                if not first:
                    a.wait_ge(s_l1, q)
                act(hT[:, 0:4, :].rearrange("p a b -> p (a b)"), pF[0:3 * F, 0, :], ACT.Copy)
                act(hT[:, 4:G, :].rearrange("p a b -> p (a b)"), pF[0:3 * F, 1, 0:(G - 4) * P],
                    ACT.Copy).then_inc(s_hTc, 1)

            def relu(q, first):
                a.wait_ge(s_l1, q + 1)
                if not first:
                    a.wait_ge(s_l2, q)
                act(r1[:, 0:4, :].rearrange("p a b -> p (a b)"), pF[:, 2, :], ACT.Relu, bias=bias1[:, 0:1])
                act(r1[:, 4:G, :].rearrange("p a b -> p (a b)"), pF[:, 3, 0:(G - 4) * P], ACT.Relu,
                    bias=bias1[:, 0:1]).then_inc(s_r1, 1)

            def root(q, b):
                a.wait_ge(s_ve, q + 1)
                act(sd[:, b, :], rs[:, b, :], ACT.Sqrt).then_inc(s_sd, 1)

            copy_h(0, True)
            relu(0, True)
            with a.Fori(0, GROUPS // 2 - 1) as m:
                copy_h(2 * m + 1, False)
                relu(2 * m + 1, False)
                root(2 * m, 0)
                copy_h(2 * m + 2, False)
                relu(2 * m + 2, False)
                root(2 * m + 1, 1)
            copy_h(GROUPS - 1, False)
            relu(GROUPS - 1, False)
            root(GROUPS - 2, 0)
            root(GROUPS - 1, 1)


_INS = {"x": "x", "src": "src", "edge": "edge_attr_32", "u": "L0_gnn_u", "W1": "L0_gnn_W1", "b1": "L0_gnn_b1",
        "W2": "L0_gnn_W2", "b2": "L0_gnn_b2"}


def kernel(**inputs):
    import numpy as np
    import concourse.bacc as bacc
    from concourse.bass_utils import run_bass_kernel_spmd

    nc = bacc.Bacc("TRN2", target_bir_lowering=False, num_devices=1)
    arrays, args = {}, {}
    for arg, name in _INS.items():
        a = np.ascontiguousarray(inputs[name])
        arrays[f"in_{name}"] = a
        args[arg] = nc.dram_tensor(f"in_{name}", a.shape, mybir.dt.from_np(a.dtype), kind="ExternalInput").ap()
    shape = tuple(inputs["x"].shape)
    out = nc.dram_tensor("out_0", shape, mybir.dt.float32, kind="ExternalOutput").ap()
    gnn_kernel(nc, out=out, **args)
    r = run_bass_kernel_spmd(nc, [arrays], core_ids=[0])
    return r.results[0]["out_0"]
```

```python
import concourse.bass as bass
from concourse import mybir
from contextlib import ExitStack

P = 128
FLT_MAX = 3.4028234663852886e38


def gnn_kernel(nc, x, src, edge, u, W1, b1, W2, b2, out):
    f32, bf16 = mybir.dt.float32, mybir.dt.bfloat16
    i32, i16 = mybir.dt.int32, mybir.dt.int16
    ALU = mybir.AluOpType
    ACT = mybir.ActivationFunctionType
    AX = mybir.AxisListType

    N, D = x.shape
    E, F = edge.shape
    H = W1.shape[1]
    NT = -(-N // P)
    NLAST = N - (NT - 1) * P
    ET = E // P
    EREST = E - ET * P
    K = 4
    STEPS = -(-(ET + 1) // K)
    J = 4
    ROUNDS = STEPS // J
    COLS = STEPS * K
    assert ROUNDS * J == STEPS and (STEPS - 1) * K == ET and EREST <= P
    PH = 2
    PR = ROUNDS // PH
    PT = COLS // PH
    PU = 2 * PR
    assert PR * PH == ROUNDS
    TH = 4
    CI = PT // ((2 * TH + 1) * K)
    CA = CI * K
    UF = TH * CI + 1
    assert PT - (2 * TH + 1) * CA == K
    R = PT
    ROWS = P * R
    EDGES = [ROWS, E - ROWS]
    SPARE = ROWS
    ZROW = ROWS + P
    NROW = ZROW + 1
    NQ = 2
    RQ = R // NQ
    CR = 2 * J
    QR = 16
    NC = QR * CR
    assert NC > NT and RQ <= 512
    CH = 104
    NCH = R // CH
    CP = 4
    FP = F // 2
    SCAN0 = PR + 2
    SCAN1 = SCAN0 + NCH * CP
    FIX0 = SCAN1 + 6
    assert FIX0 + 6 < ROUNDS - 1
    assert NCH * CH == R and NCH * CP == NQ * QR and NCH % 4 == 0 and SCAN1 + 8 < ROUNDS
    G = 7
    GROUPS = NT // G
    GP = GROUPS // 2
    PIECES = ((0, 4), (4, G))
    assert GROUPS * G == NT and GROUPS % 2 == 0

    rows_dram = [nc.dram_tensor(f"sorted_rows{h}", [ROWS, F], f32, kind="Internal").ap() for h in range(PH)]
    scan_dram = [nc.dram_tensor(f"scanned_rows{h}", [ROWS + P + 2, 2 * F], f32, kind="Internal").ap()
                 for h in range(PH)]

    ctx = ExitStack()
    with ctx:
        def sb(name, shape, dt):
            return ctx.enter_context(nc.sbuf_tensor(name, shape, dt))

        def pb(name, shape, dt):
            return ctx.enter_context(nc.psum_tensor(name, shape, dt))

        def sem(name):
            return ctx.enter_context(nc.semaphore(name))

        idf = sb("idf", [P, P], f32)
        idb = sb("idb", [P, P], bf16)
        iota32 = sb("iota32", [P, R], i32)
        iota16 = sb("iota16", [P, R], i16)
        iota_b = sb("iota_b", [P, P], bf16)
        iotak32 = sb("iotak32", [P, P, K], i32)
        iotak = sb("iotak", [P, P, K], bf16)
        before = sb("before", [P, P], f32)
        late = sb("late", [P, K, P], bf16)
        prow = sb("prow", [P, 1], i32)
        prowf = sb("prowf", [P, 1], f32)
        zeros = sb("zeros", [P, P], f32)
        ones = sb("ones", [P, NT], f32)
        neutral = sb("neutral", [1, 2 * F], f32)
        w1 = sb("w1", [3 * F, H], f32)
        w1u = sb("w1u", [P, 1], f32)
        ucol = sb("ucol", [P, 1], f32)
        b1c = sb("b1c", [P, 1], f32)
        bias1 = sb("bias1", [P, 1], f32)
        w2 = sb("w2", [H, D], f32)
        b2b = sb("b2b", [P, D], f32)
        keys = sb("keys", [P, 2, COLS], bf16)
        negk = sb("negk", [P, 2, CA], f32)
        oh_lo = sb("oh_lo", [P, J, P, K], bf16)
        oh_hi = sb("oh_hi", [P, J, NT, K], bf16)
        cn_lo = sb("cn_lo", [P, J, P, K], bf16)
        cn_hi = sb("cn_hi", [P, J, NT, K], bf16)
        loT = sb("loT", [P, 2, K, P], bf16)
        loTf = sb("loTf", [P, 2, K, P], f32)
        earlier = sb("earlier", [P, 2, K, P], bf16)
        table = sb("table", [P, 2, NT], f32)
        picked = sb("picked", [P, K, NT], f32)
        posf = sb("posf", [P, 2, K], f32)
        pos = sb("pos", [P, J, K], i32)
        feat = sb("feat", [P, J, K, F], f32)
        cnt = sb("cnt", [P, PH, NT], f32)
        incl = sb("incl", [P, NT], f32)
        start = sb("start", [P, NT], f32)
        quo = sb("quo", [P, NT], f32)
        tmpn = sb("tmpn", [P, NT], f32)
        rcnt = sb("rcnt", [P, NT], f32)
        endf = sb("endf", [P, NT], f32)
        endi = sb("endi", [P, PH, NT], i32)
        off = sb("off", [P, 1], f32)
        first_q = sb("first_q", [P, NC], f32)
        first_r = sb("first_r", [P, NQ, NC], f32)
        flat_r = first_r[:].rearrange("p q c -> p (q c)")
        zb = sb("zb", [P, RQ], bf16)
        ohq = sb("ohq", [P, 2, P], bf16)
        ohr = sb("ohr", [P, 2, RQ], bf16)
        keep = sb("keep", [P, PH, R], f32)
        keepm = sb("keepm", [P, PH, R], f32)
        tmpr = sb("tmpr", [P, R], f32)
        xs = sb("xs", [P, 2, CH, F], f32)
        sc = sb("sc", [P, 2, CH, 2 * F], f32)
        t1 = sb("t1", [P, 8], f32)
        fixi = sb("fixi", [P, PH], i32)
        nf = sb("nf", [P, 2 * F], f32)
        tail = sb("tail", [P, 2 * F], f32)
        tailT = sb("tailT", [2 * F, P], f32)
        nfT = sb("nfT", [2 * F, P], f32)
        chain = sb("chain", [2 * F, P + 1], f32)
        carry = sb("carry", [P, 2 * F], f32)
        fixg = sb("fixg", [P, 2 * F], f32)
        fixo = sb("fixo", [P, 2 * F], f32)
        xn = sb("xn", [P, NT, D], f32)
        ga = sb("ga", [P, 2, G], i32)
        gb = sb("gb", [P, 2, G], i32)
        gs = sb("gs", [P, 2, G, 2 * F], f32)
        h0 = sb("h0", [P, NT, 2 * F], f32)
        sflat = sc[:].rearrange("p a b c -> p (a b c)")
        srck = sflat[:, 0:COLS].bitcast(i32)
        ki = sflat[:, COLS:2 * COLS].bitcast(i32)
        flat = xs[:].rearrange("p a b c -> p (a b c)")
        NH, NY, NP = 2 * G * 3 * F, 2 * G * D, G * P
        h = flat[:, 0:NH].rearrange("p (a g f) -> p a g f", a=2, g=G)
        y = flat[:, NH:NH + NY].rearrange("p (a g f) -> p a g f", a=2, g=G)
        hT = flat[0:3 * F, NH + NY:NH + NY + NP].rearrange("p (g n) -> p g n", g=G)
        r1 = flat[:, NH + NY + NP:NH + NY + 2 * NP].rearrange("p (g n) -> p g n", g=G)
        st = sb("st", [P, 2, G, 6], f32)
        mv = sb("mv", [P, 2, G, 2], f32)
        rs = sb("rs", [P, 2, G], f32)
        sd = sb("sd", [P, 2, G], f32)
        root1 = sb("root1", [P, 1], f32)

        banks = pb("banks", [P, 8, 512], f32)
        pC = banks[:, 0, :]
        C = pC[:, 0:NT]
        pG = banks[:, 1:3, :]
        pE = banks[:, 3, :].rearrange("p (k n) -> p k n", k=K)
        pT = [banks[:, b, :].bitcast(bf16)[:, 0:K * P].rearrange("p (k n) -> p k n", k=K) for b in (4, 5)]
        pQ = banks[:, 6, 0:RQ]
        pN = banks[:, 7, 0:NT]
        pX = banks[:, 7, :].rearrange("p (k n) -> p k n", k=4)
        pF = banks[:, 4:8, :]

        s_const = sem("s_const")
        s_castc = sem("s_castc")
        s_src = [sem(f"s_src{h}") for h in range(PH)]
        s_fill = sem("s_fill")
        s_w = sem("s_w")
        s_xn = sem("s_xn")
        s_xz = sem("s_xz")
        s_xb = sem("s_xb")
        s_init = sem("s_init")
        s_nk = sem("s_nk")
        s_abs = sem("s_abs")
        s_oha = sem("s_oha")
        s_ca = sem("s_ca")
        s_oh1 = sem("s_oh1")
        s_cnt = sem("s_cnt")
        s_tot = sem("s_tot")
        s_off = sem("s_off")
        s_start = sem("s_start")
        s_oh = sem("s_oh")
        s_T = sem("s_T")
        s_loT = sem("s_loT")
        s_loTf = sem("s_loTf")
        s_eq = sem("s_eq")
        s_earl = sem("s_earl")
        s_seed = sem("s_seed")
        s_C = sem("s_C")
        s_tab = sem("s_tab")
        s_G = sem("s_G")
        s_pick = sem("s_pick")
        s_pos = sem("s_pos")
        s_feat = [sem(f"s_feat{j}") for j in range(J)]
        s_scat = [sem(f"s_scat{j}") for j in range(J)]
        s_ohr = sem("s_ohr")
        s_flag = sem("s_flag")
        s_keep = sem("s_keep")
        s_xs = [sem(f"s_xs{b}") for b in range(2)]
        s_open = sem("s_open")
        s_half = sem("s_half")
        s_sc = sem("s_sc")
        s_so = [sem(f"s_so{b}") for b in range(2)]
        s_nf = sem("s_nf")
        s_trT = sem("s_trT")
        s_ch = sem("s_ch")
        s_cT = sem("s_cT")
        s_fi = sem("s_fi")
        s_fg = sem("s_fg")
        s_fo = sem("s_fo")
        s_fs = sem("s_fs")
        s_v = sem("s_v")
        s_ga = sem("s_ga")
        s_h0 = sem("s_h0")
        s_gi = sem("s_gi")
        s_comb = sem("s_comb")
        s_g = [sem(f"s_g{b}") for b in range(2)]
        s_mean = sem("s_mean")
        s_hT = sem("s_hT")
        s_hTc = sem("s_hTc")
        s_l1 = sem("s_l1")
        s_r1 = sem("s_r1")
        s_l2 = sem("s_l2")
        s_y = sem("s_y")
        s_st = sem("s_st")
        s_mv = sem("s_mv")
        s_ve = sem("s_ve")
        s_sd = sem("s_sd")
        s_rs = sem("s_rs")
        s_yn = sem("s_yn")
        s_out = [sem(f"s_out{b}") for b in range(2)]

        block = ctx.enter_context(nc.Block())

        edge_t = edge[0:ET * P, :].rearrange("(p t) f -> p t f", t=ET)
        rows_p = [a.rearrange("(p r) f -> p r f", r=R) for a in rows_dram]
        scan_p = [a[0:ROWS, :].rearrange("(p r) f -> p r f", r=R) for a in scan_dram]
        x_t = x[0:(NT - 1) * P, :].rearrange("(t p) d -> p t d", p=P)
        out_t = out[0:(NT - 1) * P, :].rearrange("(t p) d -> p t d", p=P)

        @block.sync
        def _(sp):
            src_t = src[0:ET * P].rearrange("(p t) -> p t", t=ET)
            sp.dma_start(srck[:, 0:PT], src_t[:, 0:PT]).then_inc(s_src[0], 16)
            sp.dma_start(srck[:, PT:ET], src_t[:, PT:ET]).then_inc(s_src[1], 16)
            sp.wait_ge(s_fill, 1)
            sp.dma_start(srck[0:EREST, ET:ET + 1],
                         src[ET * P:E].rearrange("(p o) -> p o", o=1)).then_inc(s_src[1], 16)

            def load_rows(i, j):
                if not (isinstance(i, int) and i == 0):
                    sp.wait_ge(s_scat[j], 16 * K * i)
                sp.dma_start(feat[:, j, :, :],
                             edge_t[:, bass.ds(K * (J * i + j), K), :]).then_inc(s_feat[j], 16)

            for j in range(J):
                load_rows(0, j)
            sp.dma_start(w1[:], W1[0:3 * F, :]).then_inc(s_w, 16)
            sp.dma_start(w1u[:], W1[3 * F:3 * F + 1, :].rearrange("o h -> h o")).then_inc(s_w, 16)
            sp.dma_start(ucol[:], u[0:1, 0:1].to_broadcast([P, 1])).then_inc(s_w, 16)
            sp.dma_start(b1c[:], b1.rearrange("(h o) -> h o", o=1)).then_inc(s_w, 16)
            sp.dma_start(w2[:], W2).then_inc(s_w, 16)
            sp.dma_start(b2b[:], b2.rearrange("(o d) -> o d", o=1).to_broadcast([P, D])).then_inc(s_w, 16)
            sp.wait_ge(s_const, 2)
            pad = ROWS - EDGES[1]
            sp.dma_start(rows_dram[1][EDGES[1]:ROWS, :].rearrange("(p k) f -> p (k f)", k=4),
                         zeros[0:pad // 4, 0:4 * F]).then_inc(s_init, 16)
            for ph in range(PH):
                sp.dma_start(scan_dram[ph][SPARE:ZROW, :], zeros[:, 0:2 * F]).then_inc(s_init, 16)
                sp.dma_start(scan_dram[ph][ZROW:NROW, :], zeros[0:1, 0:2 * F]).then_inc(s_init, 16)
                sp.dma_start(scan_dram[ph][NROW:NROW + 1, :], neutral[:]).then_inc(s_init, 16)
            sp.wait_ge(s_xz, 1)
            sp.dma_start(xn[:, 0:NT - 1, :], x_t).then_inc(s_xn, 16)
            sp.dma_start(xn[0:NLAST, NT - 1, :], x[(NT - 1) * P:N, :]).then_inc(s_xn, 16)
            def rounds_rows(a, n):
                with sp.Fori(0, n) as i:
                    for j in range(J):
                        load_rows(a + i, j)

            def load_chunk(k, b, ph):
                sp.dma_start(xs[:, b, :, :], rows_p[ph][:, bass.ds(k * CH, CH), :]).then_inc(s_xs[b], 16)

            def store_chunk(k, b, ph):
                sp.wait_ge(s_sc, NCH * ph + k + 1)
                sp.dma_start(scan_p[ph][:, bass.ds(k * CH, CH), :], sc[:, b, :, :]).then_inc(s_so[b], 16)

            rounds_rows(1, SCAN0 - 1)
            for j in range(J):
                sp.wait_ge(s_scat[j], 16 * K * PR)
            load_chunk(0, 0, 0)
            load_chunk(1, 1, 0)
            rounds_rows(SCAN0, CP + 1)

            def around(k, m, b):
                store_chunk(k, b, 0)
                rounds_rows(SCAN0 + CP + 1 + CP * k, 2)
                sp.wait_ge(s_so[b], 16 * (m + 1))
                load_chunk(k + 2, b, 0)
                rounds_rows(SCAN0 + CP + 3 + CP * k, CP - 2)

            with sp.Fori(0, NCH // 2 - 1) as m:
                around(2 * m, m, 0)
                around(2 * m + 1, m, 1)
            store_chunk(NCH - 2, 0, 0)
            rounds_rows(SCAN1 - CP + 1, CP)
            store_chunk(NCH - 1, 1, 0)
            rounds_rows(SCAN1 + 1, ROUNDS - 2 - SCAN1)
            for j in range(J - 1):
                load_rows(ROUNDS - 1, j)
            j = J - 1
            sp.wait_ge(s_scat[j], 16 * K * (ROUNDS - 1))
            sp.dma_start(feat[0:EREST, j, 0, :], edge[ET * P:E, :]).then_inc(s_feat[j], 16)

            sp.wait_ge(s_init, 16 * (1 + 3 * PH))
            for j in range(J):
                sp.wait_ge(s_scat[j], 16 * K * ROUNDS if j < J - 1 else 16 * (K * (ROUNDS - 1) + 1))
            load_chunk(0, 0, 1)
            load_chunk(1, 1, 1)
            with sp.Fori(0, NCH // 2 - 1) as m:
                store_chunk(2 * m, 0, 1)
                load_chunk(2 * m + 2, 0, 1)
                store_chunk(2 * m + 1, 1, 1)
                load_chunk(2 * m + 3, 1, 1)
            store_chunk(NCH - 2, 0, 1)
            store_chunk(NCH - 1, 1, 1)

            def store_group(g, b):
                sp.wait_ge(s_yn, g + 1)
                sp.dma_start(out_t[:, bass.ds(g * G, G), :], y[:, b, :, :]).then_inc(s_out[b], 16)

            with sp.Fori(0, GP - 1) as m:
                store_group(2 * m, 0)
                store_group(2 * m + 1, 1)
            store_group(GROUPS - 2, 0)
            sp.wait_ge(s_yn, GROUPS)
            sp.dma_start(out_t[:, NT - G:NT - 1, :], y[:, 1, 0:G - 1, :]).then_inc(s_out[1], 16)
            sp.dma_start(out[(NT - 1) * P:N, :], y[0:NLAST, 1, G - 1, :]).then_inc(s_out[1], 16)
            sp.wait_ge(s_out[0], 16 * GP)
            sp.wait_ge(s_out[1], 16 * (GP + 1))

        @block.gpsimd
        def _(g):
            nc.gpsimd.memset(zeros[:], 0.0).then_inc(s_const, 1)
            nc.gpsimd.memset(neutral[:, 0:F], 0.0)
            nc.gpsimd.memset(neutral[:, F:2 * F], -FLT_MAX).then_inc(s_const, 1)
            g.iota(iotak32[:], pattern=[[1, P], [0, K]], base=0, channel_multiplier=0).then_inc(s_const, 1)
            nc.gpsimd.memset(ones[:], 1.0).then_inc(s_const, 1)
            g.iota(iota32[:], pattern=[[1, R]], base=0, channel_multiplier=0).then_inc(s_const, 1)
            g.iota(prow[:], pattern=[[1, 1]], base=0, channel_multiplier=1).then_inc(s_const, 1)
            nc.gpsimd.memset(idf[:], 0.0).then_inc(s_const, 1)
            nc.gpsimd.memset(before[:], 1.0).then_inc(s_const, 1)
            nc.gpsimd.memset(late[:], -1.0).then_inc(s_const, 1)
            nc.gpsimd.memset(zb[:], 0.0).then_inc(s_const, 1)
            g.wait_ge(s_const, 10)
            g.affine_select(out=idf[:], in_=idf[:], compare_op=ALU.not_equal, fill=1.0, base=0,
                            pattern=[[-1, P]], channel_multiplier=1).then_inc(s_const, 1)
            g.affine_select(out=before[:], in_=before[:], compare_op=ALU.is_gt, fill=0.0, base=0,
                            pattern=[[1, P]], channel_multiplier=-1).then_inc(s_const, 1)
            g.affine_select(out=late[:], in_=late[:], compare_op=ALU.is_ge, fill=0.0, base=0,
                            pattern=[[0, K], [-1, P]], channel_multiplier=1).then_inc(s_const, 1)
            nc.gpsimd.memset(xn[:, NT - 1, :], 0.0).then_inc(s_xz, 1)
            g.wait_ge(s_w, 96)
            g.wait_ge(s_xn, 32)
            nc.gpsimd.tensor_tensor(xn[:], xn[:], b2b[:].unsqueeze(1).to_broadcast([P, NT, D]),
                                    ALU.add).then_inc(s_xb, 1)

            def scatter(i, j, ph, tiles=K, parts=P):
                g.wait_ge(s_feat[j], 16 * (i + 1))
                g.wait_ge(s_pos, J * i + j + 1)
                g.nop(nofuse=True)
                for k in range(tiles):
                    g.indirect_dma_start(rows_dram[ph], bass.IndirectOffsetOnAxis(pos[0:parts, j, k:k + 1], 0),
                                         feat[0:parts, j, k, :], None).then_inc(s_scat[j], 16)

            with g.Fori(0, PR) as i:
                for j in range(J):
                    scatter(i, j, 0)
            def rounds(a, b):
                with g.Fori(a, b) as i:
                    for j in range(J):
                        scatter(i, j, 1)

            def fix_read(ph):
                g.wait_ge(s_init, 16 * (1 + 3 * PH))
                g.wait_ge(s_so[0], 16 * (ph + 1) * NCH // 2)
                g.wait_ge(s_so[1], 16 * (ph + 1) * NCH // 2)
                g.wait_ge(s_fi, ph + 1)
                g.indirect_dma_start(fixg[:], None, scan_dram[ph],
                                     bass.IndirectOffsetOnAxis(fixi[:, ph:ph + 1], 0)).then_inc(s_fg, 16)

            def fix_write(ph):
                g.wait_ge(s_fo, ph + 1)
                g.indirect_dma_start(scan_dram[ph], bass.IndirectOffsetOnAxis(fixi[:, ph:ph + 1], 0),
                                     fixo[:], None).then_inc(s_fs, 16)

            rounds(PR, FIX0)
            fix_read(0)
            rounds(FIX0, FIX0 + 6)
            fix_write(0)
            rounds(FIX0 + 6, ROUNDS - 1)
            for j in range(J - 1):
                scatter(ROUNDS - 1, j, 1)
            scatter(ROUNDS - 1, J - 1, 1, 1, EREST)

            def gather(q, b, ph, numbers, ready, free, n):
                if n is not None:
                    g.wait_ge(free, n)
                g.wait_ge(ready, q + 1)
                g.nop(nofuse=True)
                for k in range(G):
                    g.indirect_dma_start(gs[:, b, k, :], None, scan_dram[ph],
                                         bass.IndirectOffsetOnAxis(numbers[:, b, k:k + 1], 0)).then_inc(s_g[b], 16)

            g.wait_ge(s_fs, 16)
            gather(0, 0, 0, ga, s_ga, s_h0, None)
            gather(1, 1, 0, ga, s_ga, s_h0, None)
            with g.Fori(1, GP) as m:
                gather(2 * m, 0, 0, ga, s_ga, s_h0, 2 * m - 1)
                gather(2 * m + 1, 1, 0, ga, s_ga, s_h0, 2 * m)
            fix_read(1)
            fix_write(1)
            g.wait_ge(s_fs, 32)
            gather(0, 0, 1, gb, s_gi, s_h0, GROUPS - 1)
            gather(1, 1, 1, gb, s_gi, s_h0, GROUPS)
            with g.Fori(1, GP) as m:
                gather(2 * m, 0, 1, gb, s_gi, s_comb, 2 * m - 1)
                gather(2 * m + 1, 1, 1, gb, s_gi, s_comb, 2 * m)

        @block.vector
        def _(v):
            order = [0]

            def then(ins):
                order[0] += 1
                ins.then_inc(s_v, 1)
                v.wait_ge(s_v, order[0])

            nc.vector.memset(srck[:, ET:COLS], NT * P).then_inc(s_fill, 1)
            v.wait_ge(s_const, 3)
            nc.vector.tensor_copy(iotak[:], iotak32[:]).then_inc(s_castc, 1)

            def split_keys(ph):
                cols = slice(ph * PT, (ph + 1) * PT)
                v.wait_ge(s_src[ph], 16 * (ph + 1))
                then(nc.vector.tensor_single_scalar(ki[:, cols], srck[:, cols], P - 1, op=ALU.bitwise_and))
                then(nc.vector.tensor_copy(keys[:, 0, cols], ki[:, cols]))
                then(nc.vector.tensor_single_scalar(ki[:, cols], srck[:, cols], 7, op=ALU.arith_shift_right))
                then(nc.vector.tensor_copy(keys[:, 1, cols], ki[:, cols]))

            split_keys(0)
            nc.vector.tensor_scalar(negk[:], keys[:, :, 0:CA], -1.0, None, ALU.mult).then_inc(s_nk, 1)
            v.wait_ge(s_castc, 1)

            def one_hots(lo, hi, c, j, m, done):
                for kind, oh, width in ((0, lo, P), (1, hi, NT)):
                    part = keys[:, kind, bass.ds(c, m * K)].rearrange("p (m k) -> p m k", m=m).unsqueeze(2)
                    if m == 1:
                        last = nc.vector.tensor_tensor(oh[:, j, :, :], part[:, 0, :, :].to_broadcast([P, width, K]),
                                                       iotak[:, 0:width, :], ALU.is_equal)
                    else:
                        last = nc.vector.tensor_tensor(
                            oh[:, j:j + m, :, :], part.to_broadcast([P, m, width, K]),
                            iotak[:, 0:width, :].unsqueeze(1).to_broadcast([P, m, width, K]), ALU.is_equal)
                last.then_inc(done, 1)

            def count_half(u, half, c, first=False, m=2):
                if not first:
                    v.wait_ge(s_cnt, u - 1)
                one_hots(cn_lo, cn_hi, c, 2 * half, m, s_oh1)

            count_half(0, 0, CA, True)
            count_half(1, 1, CA + 2 * K, True)
            v.wait_ge(s_const, 13)
            nc.vector.tensor_copy(iota_b[:], iota32[:, 0:P]).then_inc(s_castc, 1)
            nc.vector.tensor_copy(iota16[:], iota32[:]).then_inc(s_castc, 1)
            nc.vector.tensor_copy(idb[:], idf[:]).then_inc(s_castc, 1)
            nc.vector.tensor_copy(prowf[:], prow[:]).then_inc(s_castc, 1)
            v.wait_ge(s_castc, 5)
            def count_turns(i, a):
                for n in range(a, TH):
                    count_half(TH * i + n, n % 2, CA + 2 * K * (TH * i + n))

            count_turns(0, 2)
            with v.Fori(1, CI) as i:
                count_turns(i, 0)
            count_half(UF - 1, (UF - 1) % 2, PT - K, m=1)

            def starts(ph):
                v.wait_ge(s_cnt, UF + PU * ph)
                then(nc.vector.tensor_copy(cnt[:, ph, :], pN))
                nc.vector.tensor_tensor_scan(incl[:], ones[:], cnt[:, ph, :], 0.0, ALU.mult, ALU.add).then_inc(s_tot, 1)
                v.wait_ge(s_tot, ph + 1)
                then(nc.vector.tensor_tensor(start[:], incl[:], cnt[:, ph, :], ALU.subtract))
                v.wait_ge(s_off, ph + 1)
                then(nc.vector.tensor_copy(off[:], pG[:, 0, 0:1]))
                nc.vector.tensor_scalar(start[:], start[:], off[:, 0:1], None, ALU.add).then_inc(s_start, 1)
                v.wait_ge(s_start, ph + 1)

            def first_rows(ph):
                then(nc.vector.tensor_scalar(quo[:], start[:], 1.0 / R, 0.5 / R - 0.5, ALU.mult, ALU.add))
                then(nc.vector.tensor_scalar(first_q[:, 0:NT], quo[:], 12582912.0, 12582912.0, ALU.add, ALU.subtract))
                then(nc.vector.memset(first_q[:, NT:NC], -1.0))
                then(nc.vector.memset(first_r[:, 0, NT:NC], -1.0))
                if EDGES[ph] < ROWS:
                    then(nc.vector.memset(first_q[0:1, NT:NT + 1], float(EDGES[ph] // R)))
                    then(nc.vector.memset(first_r[0:1, 0, NT:NT + 1], float(EDGES[ph] % R)))
                then(nc.vector.scalar_tensor_tensor(out=first_r[:, 0, 0:NT], in0=first_q[:, 0:NT], scalar=-float(R),
                                                    in1=start[:], op0=ALU.mult, op1=ALU.add))
                for q in range(1, NQ):
                    then(nc.vector.tensor_scalar(first_r[:, q, :], first_r[:, 0, :], -float(q * RQ), None, ALU.add))
                v.sem_inc(s_keep, 1)

            def end_rows(ph):
                then(nc.vector.scalar_tensor_tensor(out=endf[:], in0=cnt[:, ph, :], scalar=-1.0, in1=start[:],
                                                    op0=ALU.add, op1=ALU.add))
                then(nc.vector.tensor_scalar(tmpn[:], cnt[:, 0, :], 0.0, float(ZROW), ALU.is_gt, ALU.add)
                     if ph else nc.vector.memset(tmpn[:], float(NROW)))
                then(nc.vector.tensor_tensor(endf[:], endf[:], tmpn[:], ALU.subtract))
                then(nc.vector.tensor_scalar(quo[:], cnt[:, ph, :], 0.0, None, ALU.is_gt))
                then(nc.vector.tensor_tensor(endf[:], endf[:], quo[:], ALU.mult))
                then(nc.vector.tensor_tensor(endf[:], endf[:], tmpn[:], ALU.add))
                then(nc.vector.tensor_copy(endi[:, ph, :], endf[:]))

            def prepare(s, j, first):
                if not first:
                    v.wait_ge(s_C, K * (s - J) + K)
                    v.wait_ge(s_pick, K * (s - J) + K)
                one_hots(oh_lo, oh_hi, K * s, j, 1, s_oh)

            def pick(s, j, first):
                v.wait_ge(s_G, s + 1)
                for k in range(K):
                    if not first:
                        v.wait_ge(s_pick, K * (s - 1) + k + 1)
                        if k == 0 and not (isinstance(s, int) and s < 2):
                            v.wait_ge(s_pos, s - 1)
                    nc.vector.scalar_tensor_tensor(
                        out=picked[:, k, :], in0=pG[:, j % 2, k * NT:(k + 1) * NT], scalar=1.0, in1=oh_hi[:, j, :, k],
                        op0=ALU.mult, op1=ALU.mult, accum_out=posf[:, j % 2, k:k + 1]).then_inc(s_pick, 1)

            def to_int(s, j, i):
                v.wait_ge(s_pick, K * (s + 1))
                if not (isinstance(i, int) and i == 0):
                    v.wait_ge(s_scat[j], 16 * K * i)
                nc.vector.tensor_copy(pos[:, j, :], posf[:, j % 2, :]).then_inc(s_pos, 1)

            def flag_column(c, n, q, ph, b):
                v.wait_ge(s_flag, n + 2 * q + 1 + ph * NQ * (NC + 2))
                nc.vector.tensor_scalar(ohq[:, b, :], iota_b[:], first_q[:, bass.ds(c, 1)], None, ALU.is_equal)
                nc.vector.tensor_scalar(ohr[:, b, :], iota16[:, 0:RQ], flat_r[:, bass.ds(n, 1)], None,
                                        ALU.is_equal).then_inc(s_ohr, 1)

            def half_marked(q, ph):
                v.wait_ge(s_flag, (NC + 2) * (q + 1) + ph * NQ * (NC + 2))
                nc.vector.tensor_scalar(keep_flat[:, bass.ds(R * ph + RQ * q, RQ)], pQ, 0.0, None,
                                        ALU.is_equal).then_inc(s_keep, 1)

            keep_flat = keep[:].rearrange("p h r -> p (h r)")
            keepm_flat = keepm[:].rearrange("p h r -> p (h r)")

            def scans(k, b, ph, kind, features):
                rows = bass.ds(R * ph + k * CH, CH)
                for f in features:
                    last = nc.vector.tensor_tensor_scan(
                        sc[:, b, :, kind * F + f], (keep_flat, keepm_flat)[kind][:, rows], xs[:, b, :, f],
                        sc[:, 1 - b, CH - 1, kind * F + f:kind * F + f + 1],
                        (ALU.mult, ALU.min)[kind], (ALU.add, ALU.max)[kind])
                return last

            def scan_opens():
                nc.vector.memset(sc[:, 1, CH - 1, 0:F], 0.0)
                nc.vector.memset(sc[:, 1, CH - 1, F:2 * F], -FLT_MAX).then_inc(s_open, 1)

            def sort_round(i, first=False, last=False, count=False, marks=None, scan=None):
                for j in range(J):
                    s = J * i + j
                    if not (last and j + 2 >= J):
                        prepare(s + 2, (j + 2) % J, first and j + 2 < J)
                    if first and j == 0:
                        split_keys(1)
                    if count and j % 2 == 0:
                        count_half(UF + 2 * i + j // 2, (UF + j // 2) % 2, PT + 2 * K * (2 * i + j // 2))
                    if marks is not None:
                        q, r, ph = marks
                        for b in range(2):
                            flag_column(CR * r + 2 * j + b, NC * q + CR * r + 2 * j + b, q, ph, b)
                    if scan is not None:
                        k, b, m, part = scan
                        if part == 0 and j == 0:
                            v.wait_ge(s_xs[b], 16 * (m + 1))
                        if j == 0 and part in (0, 2):
                            v.wait_ge(s_open, 1)
                            v.wait_ge(s_half, 2 * k + 1 + part // 2)
                        n = FP // J
                        f0 = FP * (part % 2) + n * j
                        done = scans(k, b, 0, part // 2, range(f0, f0 + n))
                        if j == J - 1 and part % 2:
                            done.then_inc(s_half, 1)
                            if part == 3:
                                v.wait_ge(s_half, 2 * k + 4)
                                v.sem_inc(s_sc, 1)
                    pick(s, j, first and j == 0)
                    to_int(s, j, i)

            prepare(0, 0, True)
            prepare(1, 1, True)
            starts(0)

            def bounds(ph):
                v.wait_ge(s_keep, (NQ + 1) * (ph + 1))
                then(nc.vector.tensor_scalar(keepm[:, ph, :], keep[:, ph, :], 2.0, -1.0, ALU.mult, ALU.add))
                then(nc.vector.tensor_scalar(keepm[:, ph, :], keepm[:, ph, :], FLT_MAX, None, ALU.mult))
                then(nc.vector.scalar_tensor_tensor(out=tmpr[:], in0=keep[:, ph, :], scalar=float(R), in1=iota32[:],
                                                    op0=ALU.mult, op1=ALU.add))
                then(nc.vector.tensor_reduce(t1[:, 0:1], tmpr[:], AX.X, ALU.min))
                then(nc.vector.tensor_scalar(t1[:, 0:1], t1[:, 0:1], float(R), None, ALU.min))
                then(nc.vector.tensor_scalar(t1[:, 1:2], prowf[:], float(R - 1), -1.0 - SPARE, ALU.mult, ALU.add))
                then(nc.vector.tensor_tensor(t1[:, 1:2], t1[:, 1:2], t1[:, 0:1], ALU.add))
                then(nc.vector.tensor_scalar(t1[:, 2:3], t1[:, 0:1], 0.0, None, ALU.is_gt))
                then(nc.vector.tensor_tensor(t1[:, 1:2], t1[:, 1:2], t1[:, 2:3], ALU.mult))
                then(nc.vector.tensor_scalar(t1[:, 3:4], prowf[:], float(SPARE), None, ALU.add))
                then(nc.vector.tensor_tensor(t1[:, 1:2], t1[:, 1:2], t1[:, 3:4], ALU.add))
                nc.vector.tensor_copy(fixi[:, ph:ph + 1], t1[:, 1:2]).then_inc(s_fi, 1)
                then(nc.vector.tensor_scalar(t1[:, 4:5], t1[:, 0:1], float(R), None, ALU.is_ge))
                then(nc.vector.tensor_scalar(t1[:, 5:6], t1[:, 4:5], 2.0, -1.0, ALU.mult, ALU.add))
                then(nc.vector.tensor_scalar(t1[:, 5:6], t1[:, 5:6], FLT_MAX, None, ALU.mult))
                then(nc.vector.tensor_copy(nf[:, 0:F], t1[:, 4:5].to_broadcast([P, F])))
                then(nc.vector.tensor_copy(nf[:, F:2 * F], t1[:, 5:6].to_broadcast([P, F])))

            def crossing(ph):
                v.wait_ge(s_sc, NCH * (ph + 1))
                nc.vector.tensor_copy(tail[:], sc[:, (NCH - 1) % 2, CH - 1, :]).then_inc(s_nf, 1)
                v.wait_ge(s_trT, ph + 1)
                then(nc.vector.tensor_copy(tailT[:], pX[0:2 * F, 0, :]))
                then(nc.vector.tensor_copy(nfT[:], pX[0:2 * F, 1, :]))
                then(nc.vector.memset(chain[:, 0:1], 0.0))
                then(nc.vector.tensor_tensor_scan(chain[0:F, 1:P + 1], nfT[0:F, :], tailT[0:F, :], 0.0,
                                                  ALU.mult, ALU.add))
                nc.vector.tensor_tensor_scan(chain[F:2 * F, 1:P + 1], nfT[F:2 * F, :], tailT[F:2 * F, :], -FLT_MAX,
                                             ALU.min, ALU.max).then_inc(s_ch, 1)
                v.wait_ge(s_cT, ph + 1)
                then(nc.vector.tensor_copy(carry[:], pX[:, 0, 0:2 * F]))

            def change(ph):
                v.wait_ge(s_fg, 16 * (ph + 1))
                nc.vector.tensor_tensor(fixo[:, 0:F], fixg[:, 0:F], carry[:, 0:F], ALU.add)
                nc.vector.tensor_tensor(fixo[:, F:2 * F], fixg[:, F:2 * F], carry[:, F:2 * F],
                                        ALU.max).then_inc(s_fo, 1)

            sort_round(0, first=True, count=True)
            first_rows(0)
            with v.Fori(0, NQ) as q:
                with v.Fori(0, QR) as r:
                    sort_round(QR * q + r + 1, count=True, marks=(q, r, 0))
                half_marked(q, 0)
            bounds(0)
            scan_opens()
            end_rows(0)
            v.wait_ge(s_w, 96)
            then(nc.vector.tensor_scalar(bias1[:], w1u[:], ucol[:, 0:1], b1c[:, 0:1], ALU.mult, ALU.add))
            with v.Fori(NQ * QR + 1, PR) as i:
                sort_round(i, count=True)
            starts(1)
            first_rows(1)
            end_rows(1)
            then(nc.vector.tensor_tensor(rcnt[:], cnt[:, 0, :], cnt[:, 1, :], ALU.add))
            then(nc.vector.tensor_scalar(rcnt[:], rcnt[:], 1.0, None, ALU.max))
            then(nc.vector.reciprocal(rcnt[:], rcnt[:]))
            v.sem_inc(s_half, 2)
            with v.Fori(PR, SCAN0) as i:
                sort_round(i)
            with v.Fori(0, NQ) as q:
                with v.Fori(0, QR // (2 * CP)) as c:
                    for n in range(2 * CP):
                        sort_round(SCAN0 + QR * q + 2 * CP * c + n, marks=(q, 2 * CP * c + n, 1),
                                   scan=((NCH // 2) * q + 2 * c + n // CP, n // CP, (NCH // 4) * q + c, n % CP))
                half_marked(q, 1)
            crossing(0)
            bounds(1)
            with v.Fori(SCAN1, FIX0 + 4) as i:
                sort_round(i)
            change(0)
            v.wait_ge(s_so[1], 16 * NCH // 2)
            scan_opens()
            v.wait_ge(s_open, 2)
            with v.Fori(FIX0 + 4, ROUNDS - 1) as i:
                sort_round(i)
            sort_round(ROUNDS - 1, last=True)

            def scan_chunk(k, b, m):
                v.wait_ge(s_xs[b], 16 * (m + 1))
                v.wait_ge(s_sc, NCH + k)
                v.wait_ge(s_so[b], 16 * m)
                scans(k, b, 1, 0, range(F))
                scans(k, b, 1, 1, range(F)).then_inc(s_sc, 1)

            with v.Fori(0, NCH // 2) as m:
                scan_chunk(2 * m, 0, NCH // 2 + m)
                scan_chunk(2 * m + 1, 1, NCH // 2 + m)
            crossing(1)
            change(1)

            def numbers(q, b):
                nc.vector.tensor_copy(gb[:, b, :], endi[:, 1, bass.ds(q * G, G)]).then_inc(s_gi, 1)

            def means(q, b, m, more):
                v.wait_ge(s_g[b], 16 * G * (GP + m + 1))
                if more:
                    numbers(q + 2, b)
                if not (isinstance(m, int) and m == 0):
                    v.wait_ge(s_hT, 2 * (q - 1))
                tiles = bass.ds(q * G, G)
                nc.vector.tensor_tensor(h[:, b, :, 0:F], gs[:, b, :, 0:F], h0[:, tiles, 0:F], ALU.add)
                nc.vector.tensor_tensor(h[:, b, :, F:2 * F], gs[:, b, :, F:2 * F], h0[:, tiles, F:2 * F],
                                        ALU.max).then_inc(s_comb, 1)
                v.wait_ge(s_comb, q + 1)
                nc.vector.tensor_tensor(h[:, b, :, 2 * F:3 * F], h[:, b, :, 0:F],
                                        rcnt[:, tiles].unsqueeze(2).to_broadcast([P, G, F]),
                                        ALU.mult).then_inc(s_mean, 1)

            def norms(q, b, m):
                v.wait_ge(s_l2, q + 1)
                if not (isinstance(m, int) and m == 0):
                    v.wait_ge(s_out[b], 16 * m)
                nc.vector.tensor_tensor(y[:, b, :, :], pC[:, 0:G * D].rearrange("p (g d) -> p g d", g=G),
                                        xn[:, bass.ds(q * G, G), :], ALU.add).then_inc(s_y, 1)
                v.wait_ge(s_y, q + 1)
                for k in range(G):
                    last = nc.vector.bn_stats(st[:, b, k, :], y[:, b, k, :])
                last.then_inc(s_st, 1)
                v.wait_ge(s_st, q + 1)
                v.nop(nofuse=True)
                for k in range(G):
                    last = nc.vector.bn_aggr(mv[:, b, k, :], st[:, b, k, :])
                last.then_inc(s_mv, 1)
                v.wait_ge(s_mv, q + 1)
                nc.vector.tensor_scalar(rs[:, b, :], mv[:, b, :, 1], 1e-5, None, ALU.add).then_inc(s_ve, 1)

            def finish(q, b):
                v.wait_ge(s_sd, q + 1)
                nc.vector.reciprocal(rs[:, b, :], sd[:, b, :]).then_inc(s_rs, 1)
                v.wait_ge(s_rs, q + 1)
                for k in range(G):
                    last = nc.vector.tensor_scalar(y[:, b, k, :], y[:, b, k, :], mv[:, b, k, 0:1],
                                                   rs[:, b, k:k + 1], ALU.subtract, ALU.mult)
                last.then_inc(s_yn, 1)

            def turn(q, b, m, more=True):
                means(q + 1, 1 - b, m + b, more)
                finish(q - 2, b)
                norms(q - 1, 1 - b, m - (1 - b))

            v.wait_ge(s_xb, 1)
            v.wait_ge(s_h0, GROUPS)
            numbers(0, 0)
            numbers(1, 1)
            means(0, 0, 0, True)
            means(1, 1, 0, True)
            means(2, 0, 1, True)
            norms(0, 0, 0)
            turn(2, 0, 1)
            turn(3, 1, 1)
            with v.Fori(2, GP - 2) as m:
                turn(2 * m, 0, m)
                turn(2 * m + 1, 1, m)
            turn(GROUPS - 4, 0, GP - 2)
            turn(GROUPS - 3, 1, GP - 2, False)
            turn(GROUPS - 2, 0, GP - 1, False)
            finish(GROUPS - 3, 1)
            norms(GROUPS - 2, 0, GP - 1)
            finish(GROUPS - 2, 0)
            norms(GROUPS - 1, 1, GP - 1)
            finish(GROUPS - 1, 1)

        @block.tensor
        def _(t):
            mm = nc.tensor.matmul
            t.wait_ge(s_const, 13)
            mm(pN, idf[:], zeros[:, 0:NT], start=True, stop=True)

            def count_half(u, half, m=2):
                t.wait_ge(s_oh1, u + 1)
                for j in range(2 * half, 2 * half + m):
                    for k in range(K):
                        last = mm(pN, cn_lo[:, j, :, k], cn_hi[:, j, :, k], start=False, stop=True,
                                  skip_group_check=True)
                last.then_inc(s_cnt, 1)

            def count_act(i):
                t.wait_ge(s_oha, i + 1)
                for k in range(K):
                    last = mm(pN, oh_lo[:, 2, :, k], oh_hi[:, 2, :, k], start=False, stop=True,
                              skip_group_check=True)
                last.then_inc(s_ca, 1)

            with t.Fori(0, CI) as i:
                for n in range(TH):
                    count_half(TH * i + n, n % 2)
                count_act(i)
            count_half(UF - 1, (UF - 1) % 2, 1)

            def seed(ph):
                t.wait_ge(s_tot, ph + 1)
                mm(pG[:, 0, 0:1], before[:], incl[:, NT - 1:NT], start=True, stop=True).then_inc(s_off, 1)
                t.wait_ge(s_start, ph + 1)
                mm(C, idf[:], start[:], start=True, stop=True).then_inc(s_seed, 1)

            def transposes(s, j, first):
                t.wait_ge(s_oh, s + 1)
                if not first:
                    t.wait_ge(s_loTf, s - 1)
                for k in range(K):
                    last = nc.tensor.transpose(pT[j % 2][:, k, :], oh_lo[:, j, :, k], idb[:])
                last.then_inc(s_T, 1)

            def matches(s, j, first):
                t.wait_ge(s_loT, s + 1)
                if not first:
                    t.wait_ge(s_earl, s)
                mm(pE, idb[:], late[:], start=True, stop=True)
                for k in range(K):
                    last = mm(pE[:, k, :], loT[:, j % 2, k, :], loT[:, j % 2, k, :], start=False, stop=True,
                              skip_group_check=True)
                last.then_inc(s_eq, 1)

            def places(s, j, k):
                n = K * s + k
                if k == 0:
                    t.wait_ge(s_loTf, s + 1)
                    t.wait_ge(s_earl, s + 1)
                t.wait_ge(s_tab, n + 1)
                mm(C, oh_lo[:, j, :, k], oh_hi[:, j, :, k], start=False, stop=True,
                   skip_group_check=True).then_inc(s_C, 1)
                if k == 0 and not (isinstance(s, int) and s < 2):
                    t.wait_ge(s_pick, K * (s - 1))
                row = pG[:, j % 2, k * NT:(k + 1) * NT]
                mm(row, loTf[:, j % 2, k, :], table[:, k % 2, :], start=True, stop=False)
                last = mm(row, earlier[:, j % 2, k, :], oh_hi[:, j, :, k], start=False, stop=True)
                if k == K - 1:
                    last.then_inc(s_G, 1)

            def flags(n, b):
                t.wait_ge(s_ohr, n + 1)
                mm(pQ, ohq[:, b, :], ohr[:, b, :], start=False, stop=True, skip_group_check=True).then_inc(s_flag, 1)

            def sort_round(i, first=False, last=False, count=False, marks=None):
                for j in range(J):
                    s = J * i + j
                    more = not (last and j == J - 1)
                    if more:
                        transposes(s + 1, (j + 1) % J, first and j == 0)
                    places(s, j, 0)
                    places(s, j, 1)
                    if more:
                        matches(s + 1, (j + 1) % J, False)
                    places(s, j, 2)
                    places(s, j, 3)
                    if count and j % 2 == 0:
                        count_half(UF + 2 * i + j // 2, (UF + j // 2) % 2)
                    if marks is not None:
                        q, r, ph = marks
                        for b in range(2):
                            flags(NC * (NQ * ph + q) + CR * r + 2 * j + b, b)

            t.wait_ge(s_castc, 5)
            transposes(0, 0, True)
            matches(0, 0, True)
            seed(0)
            mm(pN, idf[:], zeros[:, 0:NT], start=True, stop=True)

            def opens(q, ph):
                t.wait_ge(s_keep, (NQ + 1) * ph + q + 1)
                mm(pQ, zb[:, 0:P], zb[:], start=True, stop=True).then_inc(s_flag, 2)

            def crossing(ph):
                t.wait_ge(s_nf, ph + 1)
                nc.tensor.transpose(pX[0:2 * F, 0, :], tail[:], idf[:])
                nc.tensor.transpose(pX[0:2 * F, 1, :], nf[:], idf[:]).then_inc(s_trT, 1)
                t.wait_ge(s_ch, ph + 1)
                nc.tensor.transpose(pX[:, 0, 0:2 * F], chain[:, 0:P], idf[0:2 * F, 0:2 * F]).then_inc(s_cT, 1)

            sort_round(0, first=True, count=True)
            with t.Fori(0, NQ) as q:
                opens(q, 0)
                with t.Fori(0, QR) as r:
                    sort_round(QR * q + r + 1, count=True, marks=(q, r, 0))
            with t.Fori(NQ * QR + 1, PR) as i:
                sort_round(i, count=True)
            seed(1)
            with t.Fori(PR, SCAN0) as i:
                sort_round(i)
            with t.Fori(0, NQ) as q:
                opens(q, 1)
                with t.Fori(0, QR) as r:
                    sort_round(SCAN0 + QR * q + r, marks=(q, r, 1))
            crossing(0)
            with t.Fori(SCAN1, ROUNDS - 1) as i:
                sort_round(i)
            sort_round(ROUNDS - 1, last=True)
            crossing(1)
            t.wait_ge(s_fo, 2)

            def turn(q, b, first):
                t.wait_ge(s_mean, q + 1)
                for c, (k0, k1) in enumerate(PIECES):
                    if not first:
                        t.wait_ge(s_hTc, 2 * q - 1 + c)
                    for k in range(k0, k1):
                        last = nc.tensor.transpose(pF[0:3 * F, c, (k - k0) * P:(k - k0 + 1) * P], h[:, b, k, :], idf[:])
                    last.then_inc(s_hT, 1)

            def layer1(q, first):
                for c, (k0, k1) in enumerate(PIECES):
                    t.wait_ge(s_hTc, 2 * q + c + 1)
                    if not first:
                        t.wait_ge(s_r1, 2 * q - 1 + c)
                    mm(pF[:, 2 + c, 0:(k1 - k0) * P], w1[:], hT[:, k0:k1, :], start=True, stop=True).then_inc(s_l1, 1)

            def layer2(q, first):
                if not first:
                    t.wait_ge(s_y, q)
                for c, (k0, k1) in enumerate(PIECES):
                    t.wait_ge(s_r1, 2 * q + c + 1)
                    for k in range(k0, k1):
                        last = mm(pC[:, k * D:(k + 1) * D], r1[:, k, :], w2[:], start=True, stop=True)
                last.then_inc(s_l2, 1)

            turn(0, 0, True)
            layer1(0, True)
            turn(1, 1, False)
            layer2(0, True)
            with t.Fori(0, GP - 1) as m:
                layer1(2 * m + 1, False)
                turn(2 * m + 2, 0, False)
                layer2(2 * m + 1, False)
                layer1(2 * m + 2, False)
                turn(2 * m + 3, 1, False)
                layer2(2 * m + 2, False)
            layer1(GROUPS - 1, False)
            layer2(GROUPS - 1, False)

        @block.scalar
        def _(a):
            act = nc.scalar.activation

            def copy_T(s, j, kind):
                t_, done = (loT, s_loT) if kind == 0 else (loTf, s_loTf)
                a.wait_ge(s_T, s + 1)
                act(t_[:, j % 2, :, :], pT[j % 2], ACT.Copy).then_inc(done, 1)

            def relu_matches(s, j):
                a.wait_ge(s_eq, s + 1)
                act(earlier[:, j % 2, :, :], pE, ACT.Relu).then_inc(s_earl, 1)

            def copy_table(n, k, seeded=0):
                if seeded:
                    a.wait_ge(s_seed, seeded)
                else:
                    a.wait_ge(s_C, n)
                act(table[:, k % 2, :], C, ACT.Copy).then_inc(s_tab, 1)

            def sort_round(i, last=False, seeded=0):
                for j in range(J):
                    s = J * i + j
                    more = not (last and j == J - 1)
                    if more:
                        copy_T(s + 1, (j + 1) % J, 0)
                    copy_table(K * s + 1, 1)
                    if more:
                        copy_T(s + 1, (j + 1) % J, 1)
                    copy_table(K * s + 2, 2)
                    if more:
                        relu_matches(s + 1, (j + 1) % J)
                    copy_table(K * s + 3, 3)
                    if more:
                        copy_table(K * s + 4, 0, seeded if j == J - 1 else 0)

            a.wait_ge(s_const, 4)
            act(root1[:], ones[:, 0:1], ACT.Sqrt)

            def count_step(i, first=False):
                if not first:
                    a.wait_ge(s_oha, i)
                for k in range(K):
                    c = bass.ds(K * i + k, 1)
                    act(loT[:, 0, k, :], iota_b[:], ACT.Abs, bias=negk[:, 0, c])
                    last = act(loT[:, 1, k, 0:NT], iota_b[:, 0:NT], ACT.Abs, bias=negk[:, 1, c])
                last.then_inc(s_abs, 1)
                a.wait_ge(s_abs, i + 1)
                if not first:
                    a.wait_ge(s_ca, i)
                act(oh_lo[:, 2, :, :], loT[:, 0, :, :].rearrange("p k n -> p n k"), ACT.Relu, bias=1.0, scale=-1.0)
                act(oh_hi[:, 2, :, :], loT[:, 1, :, 0:NT].rearrange("p k n -> p n k"), ACT.Relu, bias=1.0,
                    scale=-1.0).then_inc(s_oha, 1)

            a.wait_ge(s_nk, 1)
            a.wait_ge(s_castc, 2)
            count_step(0, True)
            with a.Fori(1, CI) as i:
                count_step(i)

            copy_T(0, 0, 0)
            copy_T(0, 0, 1)
            relu_matches(0, 0)
            copy_table(0, 0, 1)
            with a.Fori(0, PR - 1) as i:
                sort_round(i)
            sort_round(PR - 1, seeded=2)
            with a.Fori(PR, ROUNDS - 1) as i:
                sort_round(i)
            sort_round(ROUNDS - 1, last=True)

            def numbers(q, b):
                act(ga[:, b, :], endi[:, 0, bass.ds(q * G, G)], ACT.Copy).then_inc(s_ga, 1)

            def keep_rows(q, b, m):
                a.wait_ge(s_g[b], 16 * G * (m + 1))
                act(h0[:, bass.ds(q * G, G), :], gs[:, b, :, :], ACT.Copy).then_inc(s_h0, 1)

            numbers(0, 0)
            numbers(1, 1)
            with a.Fori(0, GP - 1) as m:
                for b in range(2):
                    keep_rows(2 * m + b, b, m)
                    numbers(2 * m + b + 2, b)
            for b in range(2):
                keep_rows(GROUPS - 2 + b, b, GP - 1)

            def copy_h(q, first):
                for c, (k0, k1) in enumerate(PIECES):
                    a.wait_ge(s_hT, 2 * q + c + 1)
                    if not first:
                        a.wait_ge(s_l1, 2 * q - 1 + c)
                    act(hT[:, k0:k1, :].rearrange("p a b -> p (a b)"), pF[0:3 * F, c, 0:(k1 - k0) * P],
                        ACT.Copy).then_inc(s_hTc, 1)

            def relu(q, first):
                if not first:
                    a.wait_ge(s_l2, q)
                for c, (k0, k1) in enumerate(PIECES):
                    a.wait_ge(s_l1, 2 * q + c + 1)
                    act(r1[:, k0:k1, :].rearrange("p a b -> p (a b)"), pF[:, 2 + c, 0:(k1 - k0) * P], ACT.Relu,
                        bias=bias1[:, 0:1]).then_inc(s_r1, 1)

            def root(q, b):
                a.wait_ge(s_ve, q + 1)
                act(sd[:, b, :], rs[:, b, :], ACT.Sqrt).then_inc(s_sd, 1)

            copy_h(0, True)
            relu(0, True)
            with a.Fori(0, GP - 1) as m:
                copy_h(2 * m + 1, False)
                relu(2 * m + 1, False)
                root(2 * m, 0)
                copy_h(2 * m + 2, False)
                relu(2 * m + 2, False)
                root(2 * m + 1, 1)
            copy_h(GROUPS - 1, False)
            relu(GROUPS - 1, False)
            root(GROUPS - 2, 0)
            root(GROUPS - 1, 1)


_INS = {"x": "x", "src": "src", "edge": "edge_attr_32", "u": "L0_gnn_u", "W1": "L0_gnn_W1", "b1": "L0_gnn_b1",
        "W2": "L0_gnn_W2", "b2": "L0_gnn_b2"}


def kernel(**inputs):
    import numpy as np
    import concourse.bacc as bacc
    from concourse.bass_utils import run_bass_kernel_spmd

    nc = bacc.Bacc("TRN2", target_bir_lowering=False, num_devices=1)
    arrays, args = {}, {}
    for arg, name in _INS.items():
        a = np.ascontiguousarray(inputs[name])
        arrays[f"in_{name}"] = a
        args[arg] = nc.dram_tensor(f"in_{name}", a.shape, mybir.dt.from_np(a.dtype), kind="ExternalInput").ap()
    shape = tuple(inputs["x"].shape)
    out = nc.dram_tensor("out_0", shape, mybir.dt.float32, kind="ExternalOutput").ap()
    gnn_kernel(nc, out=out, **args)
    r = run_bass_kernel_spmd(nc, [arrays], core_ids=[0])
    return r.results[0]["out_0"]
```
